# Optimizing a Trainium2 kernel written in Bass

```python
import numpy as np
import jax
import jax.numpy as jnp

def _softmax(x, axis=-1):
    return jax.nn.softmax(x, axis=axis)

def _gelu(x):
    return jax.nn.gelu(x, approximate=True)

def _silu(x):
    return jax.nn.silu(x)

def _sigmoid(x):
    return jax.nn.sigmoid(x)

def _layernorm(x, axis=-1, eps=1e-05):
    m = jnp.mean(x, axis=axis, keepdims=True)
    v = jnp.var(x, axis=axis, keepdims=True)
    return (x - m) / jnp.sqrt(v + eps)

def _scatter_add(tgt, idx, src, axis=0):
    return tgt.at[idx].add(src)

def _segment_sum(src, seg, n):
    return jax.ops.segment_sum(src, seg, n)
kernel_name = 'mk_decoder_postln_d2_seqx_r8_a44d4e'

def setup_inputs(seed: int=0):
    np.random.seed(seed)
    _w = jnp.asarray

    def _rec_inputs():
        import jax
        import jax.numpy as jnp
        _rk = jax.random.key(seed)
        x = -0.0002928 + 1 * jax.random.normal(jax.random.fold_in(_rk, 1), (32, 128, 128), jnp.float32)
        _lenS = 128 - jax.random.randint(jax.random.fold_in(_rk, 7), (32,), 0, max(1, 128 // 4) + 1, jnp.int32)
        _lenS2 = 128 - jax.random.randint(jax.random.fold_in(_rk, 8), (32,), 0, max(1, 128 // 4) + 1, jnp.int32)
        _ctx_1024P = jax.random.normal(jax.random.fold_in(_rk, 11), (32, 16, 128), jnp.float32)
        _ctx_1024c = jax.random.dirichlet(jax.random.fold_in(_rk, 511), 0.3 * jnp.ones((16,), jnp.float32), (32, 128))
        _ctx_1024t = jnp.einsum('bsk,bkd->bsd', _ctx_1024c, _ctx_1024P)
        _ctx_1024t = _ctx_1024t * jax.lax.rsqrt(jnp.mean(jnp.square(_ctx_1024t)) + 1e-12) * 0.953939
        ctx_1024 = -1.39393e-06 + 0.999914 * (_ctx_1024t + 0.3 * jax.random.normal(jax.random.fold_in(_rk, 611), (32, 128, 128), jnp.float32))
        _validS = jnp.arange(128)[None, :] < _lenS[:, None]
        _validS2 = jnp.arange(128)[None, :] < _lenS2[:, None]
        _causal = jnp.tril(jnp.ones((128, 128), dtype=bool))
        mask_BxS2_bk0 = jnp.logical_not(jnp.broadcast_to(_validS2[:, :], (32, 128)))
        mask_Bx1xSxS2_ik1 = jnp.where(jnp.broadcast_to(_validS2[:, None, None, :], (32, 1, 128, 128)), 1, 0).astype(jnp.int32)
        return (x, ctx_1024, mask_BxS2_bk0, mask_Bx1xSxS2_ik1)
    x, ctx_1024, mask_BxS2_bk0, mask_Bx1xSxS2_ik1 = _rec_inputs()

    def _L0_attn_setup():
        import jax, jax.numpy as jnp
        import numpy as np
        from jax import lax
        SHIFT = 1
        GAMMA = 0.25

        def q_shift_1d(x, shift=SHIFT, gamma=GAMMA):
            B, T, C = x.shape
            c1 = int(C * gamma)
            c2 = int(C * gamma * 2)
            fwd = jnp.pad(x[:, :T - shift, :c1], ((0, 0), (shift, 0), (0, 0)))
            bwd = jnp.pad(x[:, shift:, c1:c2], ((0, 0), (0, shift), (0, 0)))
            return jnp.concatenate([fwd, bwd, x[:, :, c2:]], axis=-1)

        def wkv_scan(w, u, k, v):
            B, T, C = k.shape
            ew = jnp.exp(w)

            def step(carry, kv):
                a, b = carry
                kt, vt = kv
                eku = jnp.exp(u + kt)
                out = (a + eku * vt) / (b + eku)
                ek = jnp.exp(kt)
                return ((a * ew + ek * vt, b * ew + ek), out)
            k_t = jnp.moveaxis(k, 1, 0)
            v_t = jnp.moveaxis(v, 1, 0)
            init = (jnp.zeros((B, C), k.dtype), jnp.zeros((B, C), k.dtype))
            _, ys = lax.scan(step, init, (k_t, v_t))
            return jnp.moveaxis(ys, 0, 1)
        key = jax.random.key(seed)
        ks = jax.random.split(key, 10)
        B, T, C = (8, 512, 128)
        s = 1.0 / np.sqrt(C)
        return {'x': jax.random.normal(ks[0], (B, T, C), jnp.float32), 'Wk': jax.random.normal(ks[1], (C, C), jnp.float32) * s, 'Wv': jax.random.normal(ks[2], (C, C), jnp.float32) * s, 'Wr': jax.random.normal(ks[3], (C, C), jnp.float32) * s, 'Wo': jax.random.normal(ks[4], (C, C), jnp.float32) * s, 'spatial_decay': jax.random.normal(ks[5], (C,), jnp.float32), 'spatial_first': jax.random.normal(ks[6], (C,), jnp.float32), 'mix_k': jax.random.uniform(ks[7], (C,), jnp.float32), 'mix_v': jax.random.uniform(ks[8], (C,), jnp.float32), 'mix_r': jax.random.uniform(ks[9], (C,), jnp.float32)}
    _L0_attn_all = _L0_attn_setup()
    _L0_attn_in = {k: v for k, v in _L0_attn_all.items() if k in ('Wk', 'Wv', 'Wr', 'Wo', 'spatial_decay', 'spatial_first', 'mix_k', 'mix_v', 'mix_r')}
    del _L0_attn_all

    def _L0_xattn_setup():
        import jax, jax.numpy as jnp
        import numpy as np
        B, S, D = (2, 256, 128)
        H, DH = (16, 64)
        INNER = H * DH
        FF = 512
        SCALE = DH ** (-0.5)
        EPS = 1e-05

        def layernorm(x, g, b):
            m = jnp.mean(x, axis=-1, keepdims=True)
            v = jnp.var(x, axis=-1, keepdims=True)
            return (x - m) * jax.lax.rsqrt(v + EPS) * g + b

        def attention(x, ctx, mask, wq, wk, wv, wo, bo):
            b, n, _ = x.shape
            j = ctx.shape[1]
            q = (x @ wq).reshape(b, n, H, DH).transpose(0, 2, 1, 3)
            k = (ctx @ wk).reshape(b, j, H, DH).transpose(0, 2, 1, 3)
            v = (ctx @ wv).reshape(b, j, H, DH).transpose(0, 2, 1, 3)
            sim = jnp.einsum('bhid,bhjd->bhij', q, k) * SCALE
            if mask is not None:
                neg = -jnp.finfo(sim.dtype).max
                sim = jnp.where(mask[:, None, None, :], neg, sim)
            attn = jax.nn.softmax(sim, axis=-1)
            out = jnp.einsum('bhij,bhjd->bhid', attn, v)
            out = out.transpose(0, 2, 1, 3).reshape(b, n, INNER)
            return out @ wo + bo
        key = jax.random.key(seed)
        ks = jax.random.split(key, 26)
        w = lambda k, shp, fan: (jax.random.normal(k, shp, jnp.float32) / np.sqrt(fan)).astype(jnp.float32)
        return {'x': jax.random.normal(ks[0], (B, S, D), jnp.float32), 'enc_output': jax.random.normal(ks[1], (B, S, D), jnp.float32), 'sa_wq': w(ks[2], (D, INNER), D), 'sa_wk': w(ks[3], (D, INNER), D), 'sa_wv': w(ks[4], (D, INNER), D), 'sa_wo': w(ks[5], (INNER, D), INNER), 'sa_bo': jnp.zeros((D,), jnp.float32), 'ca_wq': w(ks[6], (D, INNER), D), 'ca_wk': w(ks[7], (D, INNER), D), 'ca_wv': w(ks[8], (D, INNER), D), 'ca_wo': w(ks[9], (INNER, D), INNER), 'ca_bo': jnp.zeros((D,), jnp.float32), 'ln1_g': jnp.ones((D,), jnp.float32), 'ln1_b': jnp.zeros((D,), jnp.float32), 'ln2_g': jnp.ones((D,), jnp.float32), 'ln2_b': jnp.zeros((D,), jnp.float32), 'ln3_g': jnp.ones((D,), jnp.float32), 'ln3_b': jnp.zeros((D,), jnp.float32), 'fc1_w': w(ks[10], (D, FF), D), 'fc1_b': jnp.zeros((FF,), jnp.float32), 'fc2_w': w(ks[11], (FF, D), FF), 'fc2_b': jnp.zeros((D,), jnp.float32), 'tgt_mask': jax.random.bernoulli(ks[12], 0.1, (B, S)), 'src_mask': jax.random.bernoulli(ks[13], 0.1, (B, S))}
    _L0_xattn_all = _L0_xattn_setup()
    _L0_xattn_in = {k: v for k, v in _L0_xattn_all.items() if k in ('sa_wq', 'sa_wk', 'sa_wv', 'sa_wo', 'sa_bo', 'ca_wq', 'ca_wk', 'ca_wv', 'ca_wo', 'ca_bo', 'ln1_g', 'ln1_b', 'ln2_g', 'ln2_b', 'ln3_g', 'ln3_b', 'fc1_w', 'fc1_b', 'fc2_w', 'fc2_b')}
    del _L0_xattn_all

    def _L0_ffn_setup():
        import jax, jax.numpy as jnp
        import numpy as np
        D_MODEL, HIDDEN, N_EXPERTS, TOP_K = (128, 256, 8, 2)
        RMS_EPS = 1e-06
        key = jax.random.key(seed)
        ks = jax.random.split(key, 6)
        B, S = (4, 256)
        return {'x': jax.random.normal(ks[0], (B, S, D_MODEL), jnp.float32), 'norm_weight': jnp.ones((D_MODEL,), jnp.float32), 'gate_w': jax.random.normal(ks[1], (N_EXPERTS, D_MODEL), jnp.float32) * 0.02, 'w1': jax.random.normal(ks[2], (N_EXPERTS, HIDDEN, D_MODEL), jnp.float32) * 0.02, 'b1': jnp.zeros((N_EXPERTS, HIDDEN), jnp.float32), 'w2': jax.random.normal(ks[3], (N_EXPERTS, D_MODEL, HIDDEN), jnp.float32) * 0.02, 'b2': jnp.zeros((N_EXPERTS, D_MODEL), jnp.float32)}
    _L0_ffn_all = _L0_ffn_setup()
    _L0_ffn_in = {k: v for k, v in _L0_ffn_all.items() if k in ('norm_weight', 'gate_w', 'w1', 'b1', 'w2', 'b2')}
    del _L0_ffn_all

    def _L1_attn_setup():
        import jax, jax.numpy as jnp
        import numpy as np
        D_MODEL = 128
        HEADS = 16
        D_K = D_MODEL // HEADS
        ROPE_BASE = 10000.0

        def _rope(x, pos_offset=0):
            S, d = (x.shape[-2], x.shape[-1])
            inv_freq = 1.0 / ROPE_BASE ** (jnp.arange(0, d, 2, dtype=jnp.float32) / d)
            pos = jnp.arange(S, dtype=jnp.float32) + pos_offset
            ang = pos[:, None] * inv_freq[None, :]
            cos, sin = (jnp.cos(ang), jnp.sin(ang))
            x1, x2 = (x[..., :d // 2], x[..., d // 2:])
            return jnp.concatenate([x1 * cos - x2 * sin, x1 * sin + x2 * cos], axis=-1)
        key = jax.random.key(seed)
        ks = jax.random.split(key, 5)
        B, S = (2, 256)
        x = jax.random.normal(ks[0], (B, S, D_MODEL), dtype=jnp.float32)
        w = lambda k: jax.random.normal(k, (D_MODEL, D_MODEL), dtype=jnp.float32) * 0.02
        z = jnp.zeros((D_MODEL,), dtype=jnp.float32)
        return {'x': x, 'Wq': w(ks[1]), 'bq': z, 'Wk': w(ks[2]), 'bk': z, 'Wv': w(ks[3]), 'bv': z, 'Wo': w(ks[4]), 'bo': z}
    _L1_attn_all = _L1_attn_setup()
    _L1_attn_in = {k: v for k, v in _L1_attn_all.items() if k in ('Wq', 'bq', 'Wk', 'bk', 'Wv', 'bv', 'Wo', 'bo')}
    del _L1_attn_all

    def _L1_xattn_setup():
        import jax, jax.numpy as jnp
        import numpy as np
        HIDDEN = 128
        HEADS = 16
        HEAD_DIM = HIDDEN // HEADS
        SCALE = HEAD_DIM ** (-0.5)
        NEG_INF = -1000000000.0

        def _split_heads(x):
            B, S, _ = x.shape
            return x.reshape(B, S, HEADS, HEAD_DIM).transpose(0, 2, 1, 3)
        key = jax.random.key(seed)
        ks = jax.random.split(key, 12)
        B, Sq, Sk = (2, 256, 256)
        inp = {'query': jax.random.normal(ks[0], (B, Sq, HIDDEN), jnp.float32), 'key': jax.random.normal(ks[1], (B, Sk, HIDDEN), jnp.float32), 'value': jax.random.normal(ks[2], (B, Sk, HIDDEN), jnp.float32), 'mask': jax.random.randint(ks[3], (B, 1, Sq, Sk), 0, 2, jnp.int32), 'Wq': jax.random.normal(ks[4], (HIDDEN, HIDDEN), jnp.float32) * 0.02, 'bq': jax.random.normal(ks[5], (HIDDEN,), jnp.float32) * 0.02, 'Wk': jax.random.normal(ks[6], (HIDDEN, HIDDEN), jnp.float32) * 0.02, 'bk': jax.random.normal(ks[7], (HIDDEN,), jnp.float32) * 0.02, 'Wv': jax.random.normal(ks[8], (HIDDEN, HIDDEN), jnp.float32) * 0.02, 'bv': jax.random.normal(ks[9], (HIDDEN,), jnp.float32) * 0.02, 'Wo': jax.random.normal(ks[10], (HIDDEN, HIDDEN), jnp.float32) * 0.02}
        return inp
    _L1_xattn_all = _L1_xattn_setup()
    _L1_xattn_in = {k: v for k, v in _L1_xattn_all.items() if k in ('Wq', 'bq', 'Wk', 'bk', 'Wv', 'bv', 'Wo')}
    del _L1_xattn_all

    def _L1_ffn_setup():
        import jax, jax.numpy as jnp
        import numpy as np
        B, S, H, F, E, K = (4, 256, 128, 448, 8, 2)
        CAP_FACTOR = 1.25

        def _moe_forward(hidden_states, gate_w, w1, w2, w3):
            b, s, h = hidden_states.shape
            dtype = hidden_states.dtype
            x = hidden_states.reshape(-1, h)
            router_logits = x @ gate_w.T
            expert_weights = jax.nn.softmax(router_logits.astype(jnp.float32), axis=1)
            _, selected_experts = jax.lax.top_k(expert_weights, K)
            top_k_idx = selected_experts.reshape(b, s, K)
            probs = expert_weights.reshape(b, s, E)
            capacity = int(s * K / E * CAP_FACTOR)
            expert_mask = jax.nn.one_hot(top_k_idx, E, dtype=jnp.int32)
            mask_fused = expert_mask.reshape(b, s * K, E)
            count_fused = jnp.cumsum(mask_fused, axis=1)
            count = count_fused.reshape(b, s, K, E)
            trunc_mask = expert_mask * (count <= capacity).astype(jnp.int32)
            combined_mask = trunc_mask.sum(axis=2)
            masked_probs = probs * combined_mask
            pos_fused = mask_fused * count_fused
            pos = pos_fused.reshape(b, s, K, E)
            combined_pos = pos.sum(axis=2) * combined_mask
            pos_in_cap = jax.nn.one_hot(combined_pos, capacity + 1, dtype=jnp.int32)
            combine_mask = masked_probs[..., None] * pos_in_cap
            combine_mask = combine_mask[..., 1:].astype(dtype)
            dispatch_mask = (combine_mask != 0).astype(dtype)
            dispatch = jnp.einsum('bsm,bsec->ebcm', hidden_states, dispatch_mask)
            h1 = jnp.einsum('ebcm,emh->ebch', dispatch, w1)
            h3 = jnp.einsum('ebcm,emh->ebch', dispatch, w3)
            expert_out = jnp.einsum('ebch,ehm->ebcm', jax.nn.silu(h1) * h3, w2)
            final = jnp.einsum('ebcm,bsec->bsm', expert_out, combine_mask)
            return final
        key = jax.random.key(seed)
        k1, k2, k3, k4, k5 = jax.random.split(key, 5)
        s_h = 1.0 / np.sqrt(H)
        s_f = 1.0 / np.sqrt(F)
        return {'hidden_states': jax.random.normal(k1, (B, S, H), dtype=jnp.float32), 'gate_w': jax.random.normal(k2, (E, H), dtype=jnp.float32) * s_h, 'w1': jax.random.normal(k3, (E, H, F), dtype=jnp.float32) * s_h, 'w2': jax.random.normal(k4, (E, F, H), dtype=jnp.float32) * s_f, 'w3': jax.random.normal(k5, (E, H, F), dtype=jnp.float32) * s_h}
    _L1_ffn_all = _L1_ffn_setup()
    _L1_ffn_in = {k: v for k, v in _L1_ffn_all.items() if k in ('gate_w', 'w1', 'w2', 'w3')}
    del _L1_ffn_all
    return {'x': x, 'ctx_1024': ctx_1024, 'mask_BxS2_bk0': mask_BxS2_bk0, 'mask_Bx1xSxS2_ik1': mask_Bx1xSxS2_ik1, 'L0_attn_Wk': _L0_attn_in['Wk'], 'L0_attn_Wv': _L0_attn_in['Wv'], 'L0_attn_Wr': _L0_attn_in['Wr'], 'L0_attn_Wo': _L0_attn_in['Wo'], 'L0_attn_spatial_decay': _L0_attn_in['spatial_decay'], 'L0_attn_spatial_first': _L0_attn_in['spatial_first'], 'L0_attn_mix_k': _L0_attn_in['mix_k'], 'L0_attn_mix_v': _L0_attn_in['mix_v'], 'L0_attn_mix_r': _L0_attn_in['mix_r'], 'L0_xattn_sa_wq': _L0_xattn_in['sa_wq'], 'L0_xattn_sa_wk': _L0_xattn_in['sa_wk'], 'L0_xattn_sa_wv': _L0_xattn_in['sa_wv'], 'L0_xattn_sa_wo': _L0_xattn_in['sa_wo'], 'L0_xattn_sa_bo': _L0_xattn_in['sa_bo'], 'L0_xattn_ca_wq': _L0_xattn_in['ca_wq'], 'L0_xattn_ca_wk': _L0_xattn_in['ca_wk'], 'L0_xattn_ca_wv': _L0_xattn_in['ca_wv'], 'L0_xattn_ca_wo': _L0_xattn_in['ca_wo'], 'L0_xattn_ca_bo': _L0_xattn_in['ca_bo'], 'L0_xattn_ln1_g': _L0_xattn_in['ln1_g'], 'L0_xattn_ln1_b': _L0_xattn_in['ln1_b'], 'L0_xattn_ln2_g': _L0_xattn_in['ln2_g'], 'L0_xattn_ln2_b': _L0_xattn_in['ln2_b'], 'L0_xattn_ln3_g': _L0_xattn_in['ln3_g'], 'L0_xattn_ln3_b': _L0_xattn_in['ln3_b'], 'L0_xattn_fc1_w': _L0_xattn_in['fc1_w'], 'L0_xattn_fc1_b': _L0_xattn_in['fc1_b'], 'L0_xattn_fc2_w': _L0_xattn_in['fc2_w'], 'L0_xattn_fc2_b': _L0_xattn_in['fc2_b'], 'L0_ffn_norm_weight': _L0_ffn_in['norm_weight'], 'L0_ffn_gate_w': _L0_ffn_in['gate_w'], 'L0_ffn_w1': _L0_ffn_in['w1'], 'L0_ffn_b1': _L0_ffn_in['b1'], 'L0_ffn_w2': _L0_ffn_in['w2'], 'L0_ffn_b2': _L0_ffn_in['b2'], 'L1_attn_Wq': _L1_attn_in['Wq'], 'L1_attn_bq': _L1_attn_in['bq'], 'L1_attn_Wk': _L1_attn_in['Wk'], 'L1_attn_bk': _L1_attn_in['bk'], 'L1_attn_Wv': _L1_attn_in['Wv'], 'L1_attn_bv': _L1_attn_in['bv'], 'L1_attn_Wo': _L1_attn_in['Wo'], 'L1_attn_bo': _L1_attn_in['bo'], 'L1_xattn_Wq': _L1_xattn_in['Wq'], 'L1_xattn_bq': _L1_xattn_in['bq'], 'L1_xattn_Wk': _L1_xattn_in['Wk'], 'L1_xattn_bk': _L1_xattn_in['bk'], 'L1_xattn_Wv': _L1_xattn_in['Wv'], 'L1_xattn_bv': _L1_xattn_in['bv'], 'L1_xattn_Wo': _L1_xattn_in['Wo'], 'L1_ffn_gate_w': _L1_ffn_in['gate_w'], 'L1_ffn_w1': _L1_ffn_in['w1'], 'L1_ffn_w2': _L1_ffn_in['w2'], 'L1_ffn_w3': _L1_ffn_in['w3']}

def reference(x, ctx_1024, mask_BxS2_bk0, mask_Bx1xSxS2_ik1, L0_attn_Wk, L0_attn_Wv, L0_attn_Wr, L0_attn_Wo, L0_attn_spatial_decay, L0_attn_spatial_first, L0_attn_mix_k, L0_attn_mix_v, L0_attn_mix_r, L0_xattn_sa_wq, L0_xattn_sa_wk, L0_xattn_sa_wv, L0_xattn_sa_wo, L0_xattn_sa_bo, L0_xattn_ca_wq, L0_xattn_ca_wk, L0_xattn_ca_wv, L0_xattn_ca_wo, L0_xattn_ca_bo, L0_xattn_ln1_g, L0_xattn_ln1_b, L0_xattn_ln2_g, L0_xattn_ln2_b, L0_xattn_ln3_g, L0_xattn_ln3_b, L0_xattn_fc1_w, L0_xattn_fc1_b, L0_xattn_fc2_w, L0_xattn_fc2_b, L0_ffn_norm_weight, L0_ffn_gate_w, L0_ffn_w1, L0_ffn_b1, L0_ffn_w2, L0_ffn_b2, L1_attn_Wq, L1_attn_bq, L1_attn_Wk, L1_attn_bk, L1_attn_Wv, L1_attn_bv, L1_attn_Wo, L1_attn_bo, L1_xattn_Wq, L1_xattn_bq, L1_xattn_Wk, L1_xattn_bk, L1_xattn_Wv, L1_xattn_bv, L1_xattn_Wo, L1_ffn_gate_w, L1_ffn_w1, L1_ffn_w2, L1_ffn_w3):
    import jax
    import jax.numpy as jnp

    def _L0_attn_ref(x, Wk, Wv, Wr, Wo, spatial_decay, spatial_first, mix_k, mix_v, mix_r):
        import jax, jax.numpy as jnp
        import numpy as np
        from jax import lax
        SHIFT = 1
        GAMMA = 0.25

        def q_shift_1d(x, shift=SHIFT, gamma=GAMMA):
            B, T, C = x.shape
            c1 = int(C * gamma)
            c2 = int(C * gamma * 2)
            fwd = jnp.pad(x[:, :T - shift, :c1], ((0, 0), (shift, 0), (0, 0)))
            bwd = jnp.pad(x[:, shift:, c1:c2], ((0, 0), (0, shift), (0, 0)))
            return jnp.concatenate([fwd, bwd, x[:, :, c2:]], axis=-1)

        def wkv_scan(w, u, k, v):
            B, T, C = k.shape
            ew = jnp.exp(w)

            def step(carry, kv):
                a, b = carry
                kt, vt = kv
                eku = jnp.exp(u + kt)
                out = (a + eku * vt) / (b + eku)
                ek = jnp.exp(kt)
                return ((a * ew + ek * vt, b * ew + ek), out)
            k_t = jnp.moveaxis(k, 1, 0)
            v_t = jnp.moveaxis(v, 1, 0)
            init = (jnp.zeros((B, C), k.dtype), jnp.zeros((B, C), k.dtype))
            _, ys = lax.scan(step, init, (k_t, v_t))
            return jnp.moveaxis(ys, 0, 1)
        B, T, C = x.shape
        xx = q_shift_1d(x)
        xk = x * mix_k + xx * (1.0 - mix_k)
        xv = x * mix_v + xx * (1.0 - mix_v)
        xr = x * mix_r + xx * (1.0 - mix_r)
        k = jnp.einsum('btc,oc->bto', xk, Wk)
        v = jnp.einsum('btc,oc->bto', xv, Wv)
        r = jnp.einsum('btc,oc->bto', xr, Wr)
        sr = jax.nn.sigmoid(r)
        wkv_out = wkv_scan(spatial_decay / T, spatial_first / T, k, v)
        return jnp.einsum('btc,oc->bto', sr * wkv_out, Wo)

    def _L0_xattn_ref(x, enc_output, sa_wq, sa_wk, sa_wv, sa_wo, sa_bo, ca_wq, ca_wk, ca_wv, ca_wo, ca_bo, ln1_g, ln1_b, ln2_g, ln2_b, ln3_g, ln3_b, fc1_w, fc1_b, fc2_w, fc2_b, tgt_mask, src_mask):
        import jax, jax.numpy as jnp
        import numpy as np
        B, S, D = (2, 256, 128)
        H, DH = (16, 64)
        INNER = H * DH
        FF = 512
        SCALE = DH ** (-0.5)
        EPS = 1e-05

        def layernorm(x, g, b):
            m = jnp.mean(x, axis=-1, keepdims=True)
            v = jnp.var(x, axis=-1, keepdims=True)
            return (x - m) * jax.lax.rsqrt(v + EPS) * g + b

        def attention(x, ctx, mask, wq, wk, wv, wo, bo):
            b, n, _ = x.shape
            j = ctx.shape[1]
            q = (x @ wq).reshape(b, n, H, DH).transpose(0, 2, 1, 3)
            k = (ctx @ wk).reshape(b, j, H, DH).transpose(0, 2, 1, 3)
            v = (ctx @ wv).reshape(b, j, H, DH).transpose(0, 2, 1, 3)
            sim = jnp.einsum('bhid,bhjd->bhij', q, k) * SCALE
            if mask is not None:
                neg = -jnp.finfo(sim.dtype).max
                sim = jnp.where(mask[:, None, None, :], neg, sim)
            attn = jax.nn.softmax(sim, axis=-1)
            out = jnp.einsum('bhij,bhjd->bhid', attn, v)
            out = out.transpose(0, 2, 1, 3).reshape(b, n, INNER)
            return out @ wo + bo
        a = attention(x, x, tgt_mask, sa_wq, sa_wk, sa_wv, sa_wo, sa_bo)
        x = layernorm(x + a, ln1_g, ln1_b)
        a = attention(x, enc_output, src_mask, ca_wq, ca_wk, ca_wv, ca_wo, ca_bo)
        x = layernorm(x + a, ln2_g, ln2_b)
        h = jax.nn.gelu(x @ fc1_w + fc1_b, approximate=False)
        ff = h @ fc2_w + fc2_b
        x = layernorm(x + ff, ln3_g, ln3_b)
        return x

    def _L0_ffn_ref(x, norm_weight, gate_w, w1, b1, w2, b2):
        import jax, jax.numpy as jnp
        import numpy as np
        D_MODEL, HIDDEN, N_EXPERTS, TOP_K = (128, 256, 8, 2)
        RMS_EPS = 1e-06
        B, S, D = x.shape
        E = gate_w.shape[0]
        t = x * jax.lax.rsqrt(jnp.mean(x * x, axis=-1, keepdims=True) + RMS_EPS) * norm_weight
        tokens = t.reshape(-1, D)
        T = tokens.shape[0]
        gate_logits = tokens @ gate_w.T
        gate_scores, expert_idx = jax.lax.top_k(gate_logits, TOP_K)
        routing_weights = jax.nn.softmax(gate_scores, axis=-1)
        combine = jnp.zeros((T, E), tokens.dtype).at[jnp.arange(T)[:, None], expert_idx].add(routing_weights)

        def body(acc, params):
            W1, B1, W2, B2, c = params
            h = jax.nn.gelu(tokens @ W1.T + B1, approximate=False)
            o = h @ W2.T + B2
            return (acc + c[:, None] * o, None)
        out, _ = jax.lax.scan(body, jnp.zeros_like(tokens), (w1, b1, w2, b2, combine.T))
        return x + out.reshape(B, S, D)

    def _L1_attn_ref(x, Wq, bq, Wk, bk, Wv, bv, Wo, bo):
        import jax, jax.numpy as jnp
        import numpy as np
        D_MODEL = 128
        HEADS = 16
        D_K = D_MODEL // HEADS
        ROPE_BASE = 10000.0

        def _rope(x, pos_offset=0):
            S, d = (x.shape[-2], x.shape[-1])
            inv_freq = 1.0 / ROPE_BASE ** (jnp.arange(0, d, 2, dtype=jnp.float32) / d)
            pos = jnp.arange(S, dtype=jnp.float32) + pos_offset
            ang = pos[:, None] * inv_freq[None, :]
            cos, sin = (jnp.cos(ang), jnp.sin(ang))
            x1, x2 = (x[..., :d // 2], x[..., d // 2:])
            return jnp.concatenate([x1 * cos - x2 * sin, x1 * sin + x2 * cos], axis=-1)
        B, S, _ = x.shape

        def split_heads(t):
            return t.reshape(B, S, HEADS, D_K).transpose(0, 2, 1, 3)
        q = split_heads(x @ Wq + bq)
        k = split_heads(x @ Wk + bk)
        v = split_heads(x @ Wv + bv)
        q = _rope(q, pos_offset=0)
        k = _rope(k, pos_offset=0)
        scores = jnp.einsum('bhqd,bhkd->bhqk', q, k) / np.sqrt(D_K).astype(np.float32)
        probs = jax.nn.softmax(scores, axis=-1)
        attn = jnp.einsum('bhqk,bhkd->bhqd', probs, v)
        out = attn.transpose(0, 2, 1, 3).reshape(B, S, D_MODEL)
        return out @ Wo + bo

    def _L1_xattn_ref(query, key, value, mask, Wq, bq, Wk, bk, Wv, bv, Wo):
        import jax, jax.numpy as jnp
        import numpy as np
        HIDDEN = 128
        HEADS = 16
        HEAD_DIM = HIDDEN // HEADS
        SCALE = HEAD_DIM ** (-0.5)
        NEG_INF = -1000000000.0

        def _split_heads(x):
            B, S, _ = x.shape
            return x.reshape(B, S, HEADS, HEAD_DIM).transpose(0, 2, 1, 3)
        B, Sq, _ = query.shape
        q = _split_heads(query @ Wq.T + bq)
        k = _split_heads(key @ Wk.T + bk)
        v = _split_heads(value @ Wv.T + bv)
        scores = jnp.einsum('bhqd,bhkd->bhqk', q, k) * SCALE
        scores = jnp.where(mask == 0, NEG_INF, scores)
        attn = jax.nn.silu(scores)
        out = jnp.einsum('bhqk,bhkd->bhqd', attn, v)
        out = out.transpose(0, 2, 1, 3).reshape(B, Sq, HIDDEN)
        return out @ Wo.T

    def _L1_ffn_ref(hidden_states, gate_w, w1, w2, w3):
        import jax, jax.numpy as jnp
        import numpy as np
        B, S, H, F, E, K = (4, 256, 128, 448, 8, 2)
        CAP_FACTOR = 1.25

        def _moe_forward(hidden_states, gate_w, w1, w2, w3):
            b, s, h = hidden_states.shape
            dtype = hidden_states.dtype
            x = hidden_states.reshape(-1, h)
            router_logits = x @ gate_w.T
            expert_weights = jax.nn.softmax(router_logits.astype(jnp.float32), axis=1)
            _, selected_experts = jax.lax.top_k(expert_weights, K)
            top_k_idx = selected_experts.reshape(b, s, K)
            probs = expert_weights.reshape(b, s, E)
            capacity = int(s * K / E * CAP_FACTOR)
            expert_mask = jax.nn.one_hot(top_k_idx, E, dtype=jnp.int32)
            mask_fused = expert_mask.reshape(b, s * K, E)
            count_fused = jnp.cumsum(mask_fused, axis=1)
            count = count_fused.reshape(b, s, K, E)
            trunc_mask = expert_mask * (count <= capacity).astype(jnp.int32)
            combined_mask = trunc_mask.sum(axis=2)
            masked_probs = probs * combined_mask
            pos_fused = mask_fused * count_fused
            pos = pos_fused.reshape(b, s, K, E)
            combined_pos = pos.sum(axis=2) * combined_mask
            pos_in_cap = jax.nn.one_hot(combined_pos, capacity + 1, dtype=jnp.int32)
            combine_mask = masked_probs[..., None] * pos_in_cap
            combine_mask = combine_mask[..., 1:].astype(dtype)
            dispatch_mask = (combine_mask != 0).astype(dtype)
            dispatch = jnp.einsum('bsm,bsec->ebcm', hidden_states, dispatch_mask)
            h1 = jnp.einsum('ebcm,emh->ebch', dispatch, w1)
            h3 = jnp.einsum('ebcm,emh->ebch', dispatch, w3)
            expert_out = jnp.einsum('ebch,ehm->ebcm', jax.nn.silu(h1) * h3, w2)
            final = jnp.einsum('ebcm,bsec->bsm', expert_out, combine_mask)
            return final
        return _moe_forward(hidden_states, gate_w, w1, w2, w3)
    x = _layernorm(x + _L0_attn_ref(x, L0_attn_Wk, L0_attn_Wv, L0_attn_Wr, L0_attn_Wo, L0_attn_spatial_decay, L0_attn_spatial_first, L0_attn_mix_k, L0_attn_mix_v, L0_attn_mix_r), axis=-1)
    x = _layernorm(x + _L0_xattn_ref(x, ctx_1024, L0_xattn_sa_wq, L0_xattn_sa_wk, L0_xattn_sa_wv, L0_xattn_sa_wo, L0_xattn_sa_bo, L0_xattn_ca_wq, L0_xattn_ca_wk, L0_xattn_ca_wv, L0_xattn_ca_wo, L0_xattn_ca_bo, L0_xattn_ln1_g, L0_xattn_ln1_b, L0_xattn_ln2_g, L0_xattn_ln2_b, L0_xattn_ln3_g, L0_xattn_ln3_b, L0_xattn_fc1_w, L0_xattn_fc1_b, L0_xattn_fc2_w, L0_xattn_fc2_b, mask_BxS2_bk0, mask_BxS2_bk0), axis=-1)
    x = _layernorm(x + _L0_ffn_ref(x, L0_ffn_norm_weight, L0_ffn_gate_w, L0_ffn_w1, L0_ffn_b1, L0_ffn_w2, L0_ffn_b2), axis=-1)
    x = _layernorm(x + _L1_attn_ref(x, L1_attn_Wq, L1_attn_bq, L1_attn_Wk, L1_attn_bk, L1_attn_Wv, L1_attn_bv, L1_attn_Wo, L1_attn_bo), axis=-1)
    x = _layernorm(x + _L1_xattn_ref(x, ctx_1024, ctx_1024, mask_Bx1xSxS2_ik1, L1_xattn_Wq, L1_xattn_bq, L1_xattn_Wk, L1_xattn_bk, L1_xattn_Wv, L1_xattn_bv, L1_xattn_Wo), axis=-1)
    x = _layernorm(x + _L1_ffn_ref(x, L1_ffn_gate_w, L1_ffn_w1, L1_ffn_w2, L1_ffn_w3), axis=-1)
    return x

_drawn_inputs = setup_inputs


def setup_inputs(seed=0):
    import zlib

    import numpy as np

    out = dict(_drawn_inputs(seed))
    spreads = {'L0_xattn_sa_bo': (0.0, 0.1),
     'L0_xattn_ca_bo': (0.0, 0.1),
     'L0_xattn_ln1_g': (1.0, 0.2),
     'L0_xattn_ln1_b': (0.0, 0.1),
     'L0_xattn_ln2_g': (1.0, 0.2),
     'L0_xattn_ln2_b': (0.0, 0.1),
     'L0_xattn_ln3_g': (1.0, 0.2),
     'L0_xattn_ln3_b': (0.0, 0.1),
     'L0_xattn_fc1_b': (0.0, 0.1),
     'L0_xattn_fc2_b': (0.0, 0.1),
     'L0_ffn_norm_weight': (1.0, 0.2),
     'L0_ffn_b1': (0.0, 0.427),
     'L0_ffn_b2': (0.0, 0.1),
     'L1_attn_bq': (0.0, 0.8),
     'L1_attn_bk': (0.0, 2.0),
     'L1_attn_bv': (0.0, 0.1),
     'L1_attn_bo': (0.0, 0.1)}
    factors = {'L0_attn_spatial_first': 153.911,
     'L1_attn_Wq': 8.0,
     'L1_attn_Wk': 8.0,
     'L1_xattn_bq': 4.566,
     'L1_xattn_bk': 3.056,
     'L1_xattn_bv': 2.936}
    for name, (base, spread) in spreads.items():
        noise = np.random.default_rng([zlib.crc32(name.encode()), seed]).standard_normal(out[name].shape)
        drawn = base * np.exp(spread * noise) if base else spread * noise
        out[name] = jnp.asarray(drawn.astype(out[name].dtype))
    for name, factor in factors.items():
        out[name] = (out[name] * factor).astype(out[name].dtype)
    return out
```

```python
from contextlib import ExitStack

import concourse.bass as bass
from concourse import mybir

F32 = mybir.dt.float32
BF16 = mybir.dt.bfloat16
ALU = mybir.AluOpType
ACT = mybir.ActivationFunctionType
AX = mybir.AxisListType

B, T, D = 32, 128, 128
NB = 4
NIT = B // NB
W = NB * T
BANK = 512
HEADS = 16
GH = 4
NG = NB * HEADS // GH
GB = HEADS // GH
INNER, DH0 = 1024, 64
DH1 = D // HEADS
NT0 = INNER // 128
FF = 512
E0, HID = 8, 256
E1, F1, CAP = 8, 448, int(T * 2 / 8 * 1.25)
FT1 = 4
FP1 = F1 // FT1
NB1 = 8
NIT1 = B // NB1
SLOTS = NB1 * CAP
EC = E1 * CAP
CHUNKS = [(0, 128), (128, 128), (256, EC - 256)]
MASKED = -1e30
LN_EPS, RMS_EPS = 1e-5, 1e-6
PRIME = 2


def done(n, per, k):
    value = n * per + (PRIME + k)
    return max(value, 1) if type(n) is int else value


def build(nc, ins, out):
    ctx = ExitStack()
    with ctx:
        def sb(name, shape, dt=F32):
            return ctx.enter_context(nc.sbuf_tensor(name, shape, dt))

        def sem(name):
            return ctx.enter_context(nc.semaphore(name))

        bank = [ctx.enter_context(nc.psum_tensor(f"bank{i}", [128, BANK], F32)) for i in range(8)]

        X = sb("X", [128, B, D])
        C = sb("C", [128, B, D])
        H = sb("H", [128, B, D])
        X4 = X[:].rearrange("p (i b) d -> p i (b d)", b=NB)
        C4 = C[:].rearrange("p (i b) d -> p i (b d)", b=NB)
        H4 = H[:].rearrange("p (i b) d -> p i (b d)", b=NB)
        ident = sb("ident", [128, 128])
        upper = sb("upper", [128, 128], BF16)
        headmask = sb("headmask", [128, HEADS])
        cosr = sb("cosr", [128, DH1])
        sinr = sb("sinr", [128, DH1])
        slot = sb("slot", [128, CAP])
        rank = sb("rank", [128, 8])
        half = sb("half", [128, NB])
        lneps = sb("lneps", [128, NB])
        rmseps = sb("rmseps", [128, NB])
        carry = sb("carry", [128, 3])
        onerow = sb("onerow", [128, 128], BF16)
        keymask = sb("keymask", [128, B * T], BF16)
        rows = {}
        for name, n in (("sa_bo", D), ("ca_bo", D), ("ln1_g", D), ("ln1_b", D), ("ln2_g", D), ("ln2_b", D),
                        ("ln3_g", D), ("ln3_b", D), ("fc2_b", D), ("norm_w", D), ("l1_bqkv", 3 * D),
                        ("l1_bo", D), ("l1x_bv", D)):
            rows[name] = sb("row_" + name, [128, n])
        cols = {}
        for name, n in (("decay", 1), ("first", 1), ("mix_k", 1), ("mix_v", 1), ("mix_r", 1), ("fc1_b", FF // 128),
                        ("b1", E0 * HID // 128), ("l1x_bq", 1), ("l1x_bk", 1)):
            cols[name] = sb("col_" + name, [128, n])
        wsmall = sb("wsmall", [128, 4 * D + 4 * D + 4 * D])
        w_rwkv = wsmall[:, 0:4 * D].rearrange("p (n o) -> p n o", n=4)
        w_l1 = wsmall[:, 4 * D:8 * D]
        w_l1x = wsmall[:, 8 * D:12 * D].rearrange("p (n o) -> p n o", n=4)
        gate0 = sb("gate0", [128, E0])
        gate1 = sb("gate1", [128, E1])
        b2_sb = sb("b2_sb", [E0, D])
        wbig = sb("wbig", [128, 8 * INNER])
        w_att = [[wbig[:, (4 * a + k) * INNER:(4 * a + k + 1) * INNER] for k in range(4)] for a in range(2)]
        w1_l1 = wbig[:, 0:E1 * F1].rearrange("p (e f) -> p e f", e=E1)
        w3_l1 = wbig[:, E1 * F1:2 * E1 * F1].rearrange("p (e f) -> p e f", e=E1)
        w2_l1 = H[:].rearrange("p b d -> p (b d)")[0:FP1, 0:E1 * FT1 * D].rearrange("p (e t m) -> p e t m", e=E1, t=FT1)
        wff = sb("wff", [128, 2 * FF + 2 * E0 * HID])
        fc1 = wff[:, 0:FF]
        fc2 = wff[:, FF:2 * FF].rearrange("p (t m) -> p t m", m=D)
        w1_l0 = wff[:, 2 * FF:2 * FF + E0 * HID].rearrange("p (e f) -> p e f", e=E0)
        w2_l0 = wff[:, 2 * FF + E0 * HID:].rearrange("p (e t m) -> p e t m", e=E0, m=D)

        res = sb("res", [128, NB, D])
        nrm = sb("nrm", [128, NB, D])
        xb = sb("xb", [128, W])
        xs = sb("xs", [128, W])
        cs = sb("cs", [128, W])
        stats = sb("stats", [128, NB1, 6])
        mv = sb("mv", [128, NB1, 2])
        var = sb("var", [128, NB1])
        rstd = sb("rstd", [128, NB1])
        mask32 = [t[0:1, :, :].rearrange("p b d -> p (b d)").bitcast(mybir.dt.int32) for t in (res, nrm)]
        mask8 = [m.bitcast(mybir.dt.uint8) for m in mask32]
        work = sb("work", [128, 18000])

        class Room:

            def __init__(self):
                self.at = 0

            def take(self, *shape, parts=128):
                n = 1
                for s in shape:
                    n *= s
                ap = work[0:parts, self.at:self.at + n]
                self.at += n
                assert self.at <= 18000, self.at
                if len(shape) > 1:
                    names = " ".join(f"a{i}" for i in range(len(shape)))
                    ap = ap.rearrange(f"p ({names}) -> p {names}", **{f"a{i}": s for i, s in enumerate(shape)})
                return ap

        loaded = {k: sem("loaded_" + k) for k in ("consts", "x", "rwkv", "mix", "ctx", "small", "attention", "ff", "mask", "rows",
                                                  "moe1_w13", "moe1_w2")}
        setup_done = sem("setup_done")
        stage_end = sem("stage_end")
        stored = sem("stored")

        primed = {"pe": [], "act": [], "dve": [], "pool": [], "sp": []}

        def signal(name, producer):
            primed[producer].append(sem(name))
            return primed[producer][-1]

        class rk:
            fetched = signal("rk_fetched", "pool")
            xT_ready = signal("rk_xT_ready", "pe")
            xT_sb = signal("rk_xT_sb", "act")
            shift_sb = signal("rk_shift_sb", "act")
            kvr_ready = signal("rk_kvr_ready", "pe")
            exps = signal("rk_exps", "act")
            kvr_used = signal("rk_kvr_used", "dve")
            gated = signal("rk_gated", "dve")
            y_ready = signal("rk_y_ready", "pe")
            res_sum = signal("rk_res_sum", "dve")
            stats = signal("rk_stats", "dve")
            rstd = signal("rk_rstd", "pool")
            normed = signal("rk_normed", "dve")

        class at:
            fetched = signal("at_fetched", "pool")
            proj_ready = signal("at_proj_ready", "pe")
            proj_used = signal("at_proj_used", "act")
            scores = signal("at_scores", "pe")
            maxes = signal("at_maxes", "dve")
            probs = signal("at_probs", "act")
            probsT = signal("at_probsT", "pe")
            probsT_sb = signal("at_probsT_sb", "act")
            pv = signal("at_pv", "pe")
            heads_sb = signal("at_heads_sb", "dve")
            out_ready = signal("at_out_ready", "pe")
            out_used = signal("at_out_used", "dve")
            xb_sb = signal("at_xb_sb", "pool")
            stats = signal("at_stats", "dve")
            rstd = signal("at_rstd", "pool")
            normed = signal("at_normed", "dve")
            affine = signal("at_affine", "pool")

        class ff:
            fetched = signal("ff_fetched", "pool")
            xT_ready = signal("ff_xT_ready", "pe")
            xT_sb = signal("ff_xT_sb", "act")
            up = signal("ff_up", "pe")
            gelu = signal("ff_gelu", "act")
            down = signal("ff_down", "pe")
            res_sum = signal("ff_res_sum", "dve")
            xb_sb = signal("ff_xb_sb", "pool")
            stats = signal("ff_stats", "dve")
            rstd = signal("ff_rstd", "pool")
            normed = signal("ff_normed", "dve")
            affine = signal("ff_affine", "pool")

        class g0:
            stats = signal("g0_stats", "dve")
            rstd = signal("g0_rstd", "pool")
            tokens = signal("g0_tokens", "dve")
            tT_ready = signal("g0_tT_ready", "pe")
            tT_sb = signal("g0_tT_sb", "act")
            logits = signal("g0_logits", "pe")
            logits_sb = signal("g0_logits_sb", "act")
            gap = signal("g0_gap", "dve")
            gap_exp = signal("g0_gap_exp", "act")
            combine = signal("g0_combine", "dve")

        class m0:
            xT_ready = signal("m0_xT_ready", "pe")
            xT_sb = signal("m0_xT_sb", "act")
            bias = signal("m0_bias", "pe")
            up = signal("m0_up", "pe")
            gelu = signal("m0_gelu", "act")
            down = signal("m0_down", "pe")
            acc = signal("m0_acc", "dve")
            stats = signal("m0_stats", "dve")
            rstd = signal("m0_rstd", "pool")
            normed = signal("m0_normed", "dve")

        class l1:
            fetched = signal("l1_fetched", "pool")
            proj_ready = signal("l1_proj_ready", "pe")
            proj_used = signal("l1_proj_used", "dve")
            roped = signal("l1_roped", "pool")
            kblk = signal("l1_kblk", "pool")
            scores = signal("l1_scores", "pe")
            maxes = signal("l1_maxes", "dve")
            probs = signal("l1_probs", "act")
            probsT = signal("l1_probsT", "pe")
            probsT_sb = signal("l1_probsT_sb", "act")
            pv = signal("l1_pv", "pe")
            heads_sb = signal("l1_heads_sb", "dve")
            out_ready = signal("l1_out_ready", "pe")
            out_used = signal("l1_out_used", "dve")
            xb_sb = signal("l1_xb_sb", "pool")
            stats = signal("l1_stats", "dve")
            rstd = signal("l1_rstd", "pool")
            normed = signal("l1_normed", "dve")

        class lx:
            fetched = signal("lx_fetched", "pool")
            mask_in_even = signal("lx_mask_in_even", "sp")
            mask_in_odd = signal("lx_mask_in_odd", "sp")
            mask_f = signal("lx_mask_f", "dve")
            proj_ready = signal("lx_proj_ready", "pe")
            proj_used = signal("lx_proj_used", "act")
            qblk = signal("lx_qblk", "pool")
            scores = signal("lx_scores", "pe")
            silu = signal("lx_silu", "act")
            masked = signal("lx_masked", "dve")
            pv = signal("lx_pv", "pe")
            heads_sb = signal("lx_heads_sb", "act")
            out_ready = signal("lx_out_ready", "pe")
            out_used = signal("lx_out_used", "dve")
            stats = signal("lx_stats", "dve")
            rstd = signal("lx_rstd", "pool")
            normed = signal("lx_normed", "dve")

        class g1:
            fetched = signal("g1_fetched", "pool")
            xT_ready = signal("g1_xT_ready", "pe")
            xT_sb = signal("g1_xT_sb", "act")
            logits = signal("g1_logits", "pe")
            logits_sb = signal("g1_logits_sb", "act")
            shifted = signal("g1_shifted", "dve")
            exps = signal("g1_exps", "act")
            chosen = signal("g1_chosen", "dve")
            counts = signal("g1_counts", "pe")
            places = signal("g1_places", "dve")

        class m1:
            onehot = signal("m1_onehot", "dve")
            combine = signal("m1_combine", "pool")
            disp = signal("m1_disp", "pe")
            disp_sb = signal("m1_disp_sb", "act")
            combT = signal("m1_combT", "pe")
            combT_sb = signal("m1_combT_sb", "dve")
            up = signal("m1_up", "pe")
            silu = signal("m1_silu", "act")
            hidden = signal("m1_hidden", "dve")
            down = signal("m1_down", "pe")
            down_sb = signal("m1_down_sb", "act")
            outT = signal("m1_outT", "pe")
            outT_sb = signal("m1_outT_sb", "act")
            y_ready = signal("m1_y_ready", "pe")
            res_sum = signal("m1_res_sum", "dve")
            stats = signal("m1_stats", "dve")
            rstd = signal("m1_rstd", "pool")
            normed = signal("m1_normed", "dve")

        def prime(eng, who):
            for s in primed[who]:
                eng.sem_inc(s, PRIME)

        def carry_wait(eng):
            if eng.engine == nc.gpsimd.engine:
                nc.gpsimd.tensor_tensor(carry[:, 0:1], carry[:, 1:2], carry[:, 1:2], ALU.add)
            else:
                nc.scalar.activation(carry[:, 2:3], carry[:, 1:2], ACT.Copy)

        def end_stage(eng, n):
            eng.drain().then_inc(stage_end, 1)
            eng.wait_ge(stage_end, 4 * (n + 1))

        def norm_stats(dve, stage, src, n):
            for b in range(n):
                nc.vector.bn_stats(stats[:, b, :], src[:, b, :])
            dve.drain()
            for b in range(n):
                last = nc.vector.bn_aggr(mv[:, b, :], stats[:, b, :])
            last.then_inc(stage.stats, 1)

        def fetch(pool, stage, pairs_, read, count):
            pool.drain()
            pool.wait_ge(read, count)
            carry_wait(pool)
            for dst, src in pairs_:
                last = nc.gpsimd.tensor_copy(dst[:, :], src)
            last.then_inc(stage.fetched, 1)

        def fetching(pool, fetch_, body, base=0):
            fetch_(0)
            with pool.Fori(0, NIT - 1) as n:
                fetch_(n + 1)
                body(n)
            body(NIT - 1)

        def inv_std(pool, stage, n, eps, source):
            nc.gpsimd.tensor_tensor(var[:, 0:n], source, eps, ALU.add)
            pool.drain()
            nc.gpsimd.tensor_tensor(rstd[:, 0:n], var[:, 0:n], half[:, 0:1].to_broadcast([128, n]), ALU.pow)\
                .then_inc(stage.rstd, 1)

        def normalize(dve, stage, dst, src, n):
            for b in range(n):
                last = nc.vector.tensor_scalar(dst[:, b, :], src[:, b, :], mv[:, b, 0:1], rstd[:, b:b + 1],
                                               ALU.subtract, ALU.mult)
            last.then_inc(stage.normed, 1)

        def row4(name):
            return rows[name][:, :].unsqueeze(1).to_broadcast([128, NB, D])

        def by4(ap):
            return ap.rearrange("p (b d) -> p b d", b=NB)

        r = Room()
        rk_scaled = r.take(3, 2, D)
        rk_onem = r.take(3)
        rk_ew = r.take(NB, T)
        rk_ewc = r.take(1)
        rk_u = r.take(1)
        rk_xT = [r.take(NB, T) for _ in range(2)]
        rk_xx = [r.take(NB, T) for _ in range(2)]
        rk_ek = [r.take(NB, T) for _ in range(2)]
        rk_eku = [r.take(NB, T) for _ in range(2)]
        rk_er = [r.take(NB, T) for _ in range(2)]
        rk_ekv = r.take(NB, T)
        rk_a = r.take(NB, T)
        rk_b = r.take(NB, T)
        rk_num = r.take(NB, T)
        rk_den = r.take(NB, T)
        rk_z = [r.take(NB, T) for _ in range(2)]

        def two_deep(eng, front, back):
            front(0, 0)
            with eng.Fori(0, (NIT - 2) // 2) as i:
                for j in (0, 1):
                    front(i * 2 + (j + 1), (j + 1) % 2)
                    back(i * 2 + j, j)
            front(NIT - 1, 1)
            back(NIT - 2, 0)
            back(NIT - 1, 1)

        def flat(ap):
            return ap.rearrange("p b t -> p (b t)")

        def rwkv_pe(pe):
            def front(n, s):
                pe.wait_ge(rk.shift_sb, done(n, 1, 0))
                pe.wait_ge(rk.fetched, done(n, 1, 1))
                for b in range(NB):
                    last = nc.tensor.transpose(bank[0][:, b * T:(b + 1) * T], xs[:, b * D:(b + 1) * D], ident[:])
                last.then_inc(rk.xT_ready, 1)
                pe.wait_ge(rk.shift_sb, done(n, 1, 1))
                pe.wait_ge(rk.kvr_used, done(n, 1, -1))
                for k in range(3):
                    o = bank[1 + 3 * s + k]
                    nc.tensor.matmul(o[:], rk_scaled[:, k, 0, :], flat(rk_xT[s]), start=True, stop=False)
                    last = nc.tensor.matmul(o[:], rk_scaled[:, k, 1, :], flat(rk_xx[s]), start=False, stop=True)
                last.then_inc(rk.kvr_ready, 1)

            def back(n, s):
                pe.wait_ge(rk.gated, done(n, 1, 1))
                pe.wait_ge(rk.res_sum, done(n, 1, 0))
                for b in range(NB):
                    last = nc.tensor.matmul(bank[7][:, b * T:(b + 1) * T], rk_z[s][:, b, :], w_rwkv[:, 3, :],
                                            start=True, stop=True)
                last.then_inc(rk.y_ready, 1)
            two_deep(pe, front, back)

        def rwkv_act(act):
            def front(n, s):
                act.wait_ge(rk.xT_ready, done(n, 1, 1))
                act.wait_ge(rk.kvr_ready, done(n, 1, -1))
                src = bank[0][:, :].rearrange("p (b t) -> p b t", b=NB)
                nc.scalar.activation(flat(rk_xT[s]), bank[0][:, :], ACT.Copy)
                nc.scalar.activation(rk_xx[s][0:32, :, 1:T], src[0:32, :, 0:T - 1], ACT.Copy)
                nc.scalar.activation(rk_xx[s][32:64, :, 0:T - 1], src[32:64, :, 1:T], ACT.Copy)
                nc.scalar.activation(rk_xx[s][64:128], src[64:128], ACT.Copy).then_inc(rk.shift_sb, 1)
                act.wait_ge(rk.kvr_ready, done(n, 1, 1))
                act.wait_ge(rk.gated, done(n, 1, -1))
                kv = [bank[1 + 3 * s + k][:, :].rearrange("p (b t) -> p b t", b=NB) for k in range(3)]
                nc.scalar.activation(rk_ek[s][:, :, 1:T], kv[0][:, :, 0:T - 1], ACT.Exp)
                nc.scalar.activation(flat(rk_eku[s]), bank[1 + 3 * s][:, :], ACT.Exp, bias=rk_u[:, 0:1])
                nc.scalar.activation(flat(rk_er[s]), bank[3 + 3 * s][:, :], ACT.Exp, scale=-1.0)\
                    .then_inc(rk.exps, 1)

            def back(n, s):
                pass
            two_deep(act, front, back)

        def rwkv_dve(dve):
            def front(n, s):
                pass

            def back(n, s):
                dve.wait_ge(rk.exps, done(n, 1, 1))
                v = bank[2 + 3 * s][:, :].rearrange("p (b t) -> p b t", b=NB)
                tt = nc.vector.tensor_tensor
                tt(rk_ekv[:, :, 1:T], rk_ek[s][:, :, 1:T], v[:, :, 0:T - 1], ALU.mult)
                nc.vector.tensor_tensor_scan(flat(rk_b), flat(rk_ew), flat(rk_ek[s]), 0.0, ALU.mult, ALU.add)
                tt(flat(rk_num), flat(rk_eku[s]), bank[2 + 3 * s][:, :], ALU.mult).then_inc(rk.kvr_used, 1)
                dve.drain()
                nc.vector.tensor_tensor_scan(flat(rk_a), flat(rk_ew), flat(rk_ekv), 0.0, ALU.mult, ALU.add)
                tt(flat(rk_b), flat(rk_b), flat(rk_eku[s]), ALU.add)
                dve.drain()
                tt(flat(rk_num), flat(rk_num), flat(rk_a), ALU.add)
                nc.vector.scalar_tensor_tensor(flat(rk_den), flat(rk_er[s]), 1.0, flat(rk_b), ALU.add, ALU.mult)
                dve.drain()
                nc.vector.reciprocal(flat(rk_den), flat(rk_den))
                dve.drain()
                dve.wait_ge(rk.y_ready, done(n, 1, -1))
                tt(flat(rk_z[s]), flat(rk_num), flat(rk_den), ALU.mult).then_inc(rk.gated, 1)
                dve.wait_ge(rk.y_ready, done(n, 1, 1))
                dve.wait_ge(rk.xT_ready, done(n, 1, 1))
                tt(res[:].rearrange("p b d -> p (b d)"), bank[7][:, :], X4[:, n, :], ALU.add)\
                    .then_inc(rk.res_sum, 1)
                dve.drain()
                norm_stats(dve, rk, res, NB)
                dve.wait_ge(rk.rstd, done(n, 1, 1))
                normalize(dve, rk, by4(X4[:, n, :]), res, NB)
                dve.drain()
            two_deep(dve, front, back)

        def rwkv_pool(pool):
            def body(n):
                pool.wait_ge(rk.stats, done(n, 1, 1))
                inv_std(pool, rk, NB, lneps[:, 0:NB], mv[:, 0:NB, 1])
            fetching(pool, lambda n: fetch(pool, rk, [(xs, X4[:, n, :])], rk.xT_ready, done(n, 1, 0)), body)

        def steps():
            for n in range(-1, NG + 3):
                ot = (n - GB - 1) // GB if (n - GB - 1) % GB == 0 and n > GB else None
                wo = (n - GB - 2) // GB if (n - GB - 2) % GB == 0 and n > GB + 1 else None
                yield (n, n + 1 if n + 1 < NG else None, n if 0 <= n < NG else None,
                       n - 1 if 1 <= n <= NG else None, ot, wo)

        def head_of(q, h, dh):
            return (q // 2) * 2 * GH + 2 * h + q % 2 if dh == DH0 else q * GH + h

        def group_of(heads, q, dh):
            if dh == DH0:
                return heads.rearrange("p (a h s d) -> p a h s d", a=2, h=GH, s=2)[:, q // 2, :, q % 2, :]
            return heads[:, q * GH * dh:(q + 1) * GH * dh].rearrange("p (h d) -> p h d", h=GH)

        S_BANK, PT_BANK, O_BANK, W_BANK = 0, 2, 4, 6

        def softmax_pe(pe, stage, n, scores, vaug, probs, probsT_sb, heads, headsT, wo, dh, wring, hook=None):
            nt = HEADS * dh // 128
            for step, g_s, g_t, g_v, b_ot, b_wo in steps():
                if g_s is not None:
                    pe.wait_ge(stage.probs, done(n, NG, g_s - 1))
                    scores(g_s)
                if b_ot is not None:
                    pe.wait_ge(stage.heads_sb, done(n, NG, (b_ot + 1) * GB))
                    for q in range(0, nt, 4):
                        o = wring(n)
                        for t in range(q, min(q + 4, nt)):
                            last = nc.tensor.transpose(o[:, (t - q) * 128:(t - q + 1) * 128],
                                                       heads[b_ot % 2][:, t * 128:(t + 1) * 128], ident[:])
                        last.then_inc(stage.out_ready, 1)
                if g_t is not None:
                    pe.wait_ge(stage.probs, done(n, NG, g_t + 1))
                    pe.wait_ge(stage.probsT_sb, done(n, NG, g_t - 1))
                    for h in range(GH):
                        last = nc.tensor.transpose(bank[PT_BANK + g_t % 2][:, h * T:(h + 1) * T],
                                                   probs[g_t % 2][:, h, :], ident[:])
                    last.then_inc(stage.probsT, 1)
                if b_wo is not None:
                    o = wring(n)
                    pe.wait_ge(stage.out_used, done(n, wring.per, wring.count - 1))
                    for t in range(nt):
                        last = nc.tensor.matmul(o[:, 0:D], headsT[:, t, :], wo[:, t * D:(t + 1) * D],
                                                start=(t == 0), stop=(t == nt - 1))
                    last.then_inc(stage.out_ready, 1)
                if g_v is not None:
                    pe.wait_ge(stage.probsT_sb, done(n, NG, g_v + 1))
                    pe.wait_ge(stage.heads_sb, done(n, NG, g_v - 1))
                    for h in range(GH):
                        last = nc.tensor.matmul(bank[O_BANK + g_v % 2][:, h * (dh + 1):(h + 1) * (dh + 1)],
                                                probsT_sb[g_v % 2][:, h, :],
                                                vaug[:, g_v // GB, head_of(g_v % GB, h, dh), :], start=True, stop=True)
                    last.then_inc(stage.pv, 1)
                if hook:
                    hook(step)

        class OutRing:

            def __init__(self, pe, stage, per, first):
                self.pe, self.stage, self.per, self.first, self.count = pe, stage, per, first, 0

            def __call__(self, n):
                if self.count < 2:
                    self.first(n, self.count)
                else:
                    self.pe.wait_ge(self.stage.out_used, done(n, self.per, self.count - 1))
                self.count += 1
                return bank[W_BANK + (self.count - 1) % 2]

        def softmax_act(act, stage, n, nmax, probs, probsT_sb, hook=None):
            def exps(g):
                act.wait_ge(stage.maxes, done(n, NG, g + 1))
                act.wait_ge(stage.probsT, done(n, NG, g - 1))
                for h in range(GH):
                    last = nc.scalar.activation(probs[g % 2][:, h, :], bank[S_BANK + g % 2][:, h * T:(h + 1) * T],
                                                ACT.Exp, bias=nmax[:, g % 4, h:h + 1])
                last.then_inc(stage.probs, 1)
            for step, g_s, g_t, g_v, b_ot, b_wo in steps():
                if g_s is not None:
                    exps(g_s)
                if g_t is not None:
                    act.wait_ge(stage.probsT, done(n, NG, g_t + 1))
                    act.wait_ge(stage.pv, done(n, NG, g_t - 1))
                    nc.scalar.activation(probsT_sb[g_t % 2].rearrange("p h t -> p (h t)"),
                                         bank[PT_BANK + g_t % 2][:, :], ACT.Copy).then_inc(stage.probsT_sb, 1)
                if hook:
                    hook(step)

        def softmax_dve(dve, stage, n, nmax, recip, heads, headsT, dh, out_per, xb_, hook=None):
            nt = HEADS * dh // 128
            used = 0
            for step, g_s, g_t, g_v, b_ot, b_wo in steps():
                if g_s is not None:
                    dve.wait_ge(stage.scores, done(n, NG, g_s + 1))
                    nc.vector.tensor_reduce(nmax[:, g_s % 4, :],
                                            bank[S_BANK + g_s % 2][:, :].rearrange("p (h t) -> p h t", h=GH),
                                            AX.X, ALU.max, negate=True).then_inc(stage.maxes, 1)
                if g_v is not None:
                    dve.wait_ge(stage.pv, done(n, NG, g_v + 1))
                    if g_v % GB == 0:
                        b = g_v // GB
                        dve.wait_ge(stage.out_ready, done(n, out_per, b * (out_per // NB) - 1 if b else 0))
                    o = bank[O_BANK + g_v % 2][:, 0:GH * (dh + 1)].rearrange("p (h d) -> p h d", h=GH)
                    nc.vector.reciprocal(recip[:, g_v % 2, :], o[:, :, dh])
                    dve.drain()
                    nc.vector.tensor_tensor(
                        group_of(heads[(g_v // GB) % 2], g_v % GB, dh),
                        o[:, :, 0:dh], recip[:, g_v % 2, :].unsqueeze(2).to_broadcast([128, GH, dh]), ALU.mult)\
                        .then_inc(stage.heads_sb, 1)
                if b_ot is not None:
                    for q in range(0, nt, 4):
                        m = min(4, nt - q)
                        dve.wait_ge(stage.out_ready, done(n, out_per, used + 1))
                        nc.vector.tensor_copy(headsT[:, q:q + m, :].rearrange("p a b -> p (a b)"),
                                              bank[W_BANK + used % 2][:, 0:m * 128])\
                            .then_inc(stage.out_used, 1)
                        used += 1
                if b_wo is not None:
                    dve.wait_ge(stage.out_ready, done(n, out_per, used + 1))
                    if b_wo == 0:
                        dve.wait_ge(stage.xb_sb, done(n, 1, 1))
                    nc.vector.tensor_tensor(res[:, b_wo, :], bank[W_BANK + used % 2][:, 0:D],
                                            xb_[:, b_wo * D:(b_wo + 1) * D], ALU.add)\
                        .then_inc(stage.out_used, 1)
                    used += 1
                if hook:
                    hook(step)
            dve.drain()

        r = Room()
        at_q = r.take(NT0, W)
        at_k = r.take(NT0, W)
        at_v = r.take(NB, HEADS, DH0 + 1)
        at_xT = r.take(W)
        at_probs = [r.take(GH, T) for _ in range(2)]
        at_probsT = [r.take(GH, T) for _ in range(2)]
        at_heads = [r.take(INNER)] * 2
        at_headsT = r.take(NT0, 128)
        at_nmax = r.take(4, GH)
        at_recip = r.take(2, GH)
        OUT0 = NB * (NT0 // 4 + 1)
        at_cT = r.take(W)

        def attention_pe(pe, a):
            base = a * NIT
            wq, wk, wv, wo = w_att[a]
            with pe.Fori(0, NIT) as i:
                n = i + base
                nproj = 2 + 2 * NT0 + 2 * NB
                count = 0

                def ring():
                    nonlocal count
                    if count < 2:
                        pe.wait_ge(at.out_used, done(n, OUT0, 0))
                        pe.wait_ge(at.proj_used, done(n, nproj, 0))
                    else:
                        pe.wait_ge(at.proj_used, done(n, nproj, count - 1))
                    count += 1
                    return bank[W_BANK + (count - 1) % 2]
                pe.wait_ge(at.fetched, done(n, 1, 1))
                for s in (xs, cs if a else xs):
                    o = ring()
                    for b in range(NB):
                        last = nc.tensor.transpose(o[:, b * T:(b + 1) * T], s[:, b * D:(b + 1) * D], ident[:])
                    last.then_inc(at.proj_ready, 1)
                pe.wait_ge(at.proj_used, done(n, nproj, 2))
                kv = at_cT
                for w, xT in ((wq, at_xT), (wk, kv)):
                    for t in range(NT0):
                        o = ring()
                        nc.tensor.matmul(o[:], w[:, t * 128:(t + 1) * 128], xT[:, :], start=True, stop=True)\
                            .then_inc(at.proj_ready, 1)
                for b in range(NB):
                    for j in range(2):
                        o = ring()
                        nc.tensor.matmul(o[:], kv[:, b * T:(b + 1) * T], wv[:, j * 512:(j + 1) * 512],
                                         start=True, stop=True).then_inc(at.proj_ready, 1)
                pe.wait_ge(at.proj_used, done(n, nproj, nproj))

                def scores(g):
                    b, o = g // GB, bank[S_BANK + g % 2]
                    nc.tensor.matmul(o[:, :].rearrange("p (h t) -> p h t", h=GH), onerow[:, :],
                                     keymask[:, :].rearrange("p (i b t) -> p i b t", i=NIT, b=NB)[:, i, b, :]
                                     .unsqueeze(1).to_broadcast([128, GH, T]), start=True, stop=False,
                                     skip_group_check=True)
                    for h in range(GH):
                        head = head_of(g % GB, h, DH0)
                        p, t = (head % 2) * DH0, head // 2
                        last = nc.tensor.matmul(o[:, h * T:(h + 1) * T], at_q[p:p + DH0, t, b * T:(b + 1) * T],
                                                at_k[p:p + DH0, t, b * T:(b + 1) * T], start=False, stop=(h == GH - 1),
                                                skip_group_check=True)
                    last.then_inc(at.scores, 1)

                wring = OutRing(pe, at, OUT0, lambda n, k: None)
                softmax_pe(pe, at, n, scores, at_v, at_probs, at_probsT, at_heads, at_headsT, wo, DH0, wring)

        def attention_act(act, a):
            base = a * NIT
            with act.Fori(0, NIT) as i:
                n = i + base
                nproj = 2 + 2 * NT0 + 2 * NB
                count = 0

                def evacuate(dst, scale=1.0):
                    nonlocal count
                    act.wait_ge(at.proj_ready, done(n, nproj, count + 1))
                    src = bank[W_BANK + count % 2][:, :]
                    if len(dst.shape) == 3:
                        src = src.rearrange("p (h d) -> p h d", d=DH0)
                    nc.scalar.activation(dst, src, ACT.Copy, scale=scale).then_inc(at.proj_used, 1)
                    count += 1
                evacuate(at_xT[:, :])
                evacuate(at_cT[:, :])
                for t in range(NT0):
                    evacuate(at_q[:, t, :], DH0 ** -0.5)
                for t in range(NT0):
                    evacuate(at_k[:, t, :])
                act.wait_ge(at.pv, done(n, NG, 0))
                for b in range(NB):
                    for j in range(2):
                        evacuate(at_v[:, b, j * 8:(j + 1) * 8, 0:DH0])
                softmax_act(act, at, n, at_nmax, at_probs, at_probsT)

        def attention_dve(dve, a):
            base = a * NIT
            with dve.Fori(0, NIT) as i:
                n = i + base
                softmax_dve(dve, at, n, at_nmax, at_recip, at_heads, at_headsT, DH0, OUT0, xb)
                norm_stats(dve, at, res, NB)
                dve.wait_ge(at.rstd, done(n, 1, 1))
                dve.wait_ge(at.affine, done(n, 1, 0))
                normalize(dve, at, nrm, res, NB)
                dve.drain()

        def attention_pool(pool, a):
            base = a * NIT
            src = X4 if a == 0 else H4
            g, b_, bo = (("ln1_g", "ln1_b", "sa_bo"), ("ln2_g", "ln2_b", "ca_bo"))[a]
            nproj = 2 + 2 * NT0 + 2 * NB

            def fetch_(i):
                fetch(pool, at, [(xs, src[:, i, :])] + [(cs, C4[:, i, :])] * a,
                      at.proj_ready, done(i + base, nproj, 2 - nproj))

            def body(i):
                n = i + base
                pool.drain()
                pool.wait_ge(at.stats, done(n, 1, 0))
                carry_wait(pool)
                nc.gpsimd.tensor_tensor(by4(xb[:, :]), by4(src[:, i, :]), row4(bo), ALU.add)\
                    .then_inc(at.xb_sb, 1)
                pool.wait_ge(at.stats, done(n, 1, 1))
                inv_std(pool, at, NB, lneps[:, 0:NB], mv[:, 0:NB, 1])
                pool.wait_ge(at.normed, done(n, 1, 1))
                nc.gpsimd.tensor_tensor(nrm[:], nrm[:], row4(g), ALU.mult)
                pool.drain()
                nc.gpsimd.tensor_tensor(by4(H4[:, i, :]), nrm[:], row4(b_), ALU.add).then_inc(at.affine, 1)
            fetching(pool, fetch_, body)

        r = Room()
        ff_xT = r.take(W)
        ff_h = r.take(FF // 128, W)
        ff_sum = r.take(NB, D)
        NFF = FF // 128

        def ffn_pe(pe):
            with pe.Fori(0, NIT) as n:
                pe.wait_ge(ff.xT_sb, done(n, 1, 0))
                pe.wait_ge(ff.fetched, done(n, 1, 1))
                for b in range(NB):
                    last = nc.tensor.transpose(bank[0][:, b * T:(b + 1) * T], xs[:, b * D:(b + 1) * D], ident[:])
                last.then_inc(ff.xT_ready, 1)
                pe.wait_ge(ff.xT_sb, done(n, 1, 1))
                pe.wait_ge(ff.gelu, done(n, NFF, 0))
                for t in range(NFF):
                    nc.tensor.matmul(bank[1 + t][:], fc1[:, t * 128:(t + 1) * 128], ff_xT[:, :],
                                     start=True, stop=True).then_inc(ff.up, 1)
                pe.wait_ge(ff.gelu, done(n, NFF, NFF))
                pe.wait_ge(ff.res_sum, done(n, 1, 0))
                for b in range(NB):
                    for t in range(NFF):
                        last = nc.tensor.matmul(bank[5][:, b * D:(b + 1) * D], ff_h[:, t, b * T:(b + 1) * T],
                                                fc2[:, t, :], start=(t == 0), stop=(t == NFF - 1))
                last.then_inc(ff.down, 1)

        def ffn_act(act):
            with act.Fori(0, NIT) as n:
                act.wait_ge(ff.xT_ready, done(n, 1, 1))
                act.wait_ge(ff.up, done(n, NFF, 0))
                nc.scalar.activation(ff_xT[:, :], bank[0][:, :], ACT.Copy).then_inc(ff.xT_sb, 1)
                act.wait_ge(ff.down, done(n, 1, 0))
                for t in range(NFF):
                    act.wait_ge(ff.up, done(n, NFF, t + 1))
                    nc.scalar.activation(ff_h[:, t, :], bank[1 + t][:, :], ACT.Gelu, bias=cols["fc1_b"][:, t:t + 1])\
                        .then_inc(ff.gelu, 1)

        def ffn_dve(dve):
            with dve.Fori(0, NIT) as n:
                dve.wait_ge(ff.down, done(n, 1, 1))
                dve.wait_ge(ff.xb_sb, done(n, 1, 1))
                nc.vector.tensor_tensor(res[:].rearrange("p b d -> p (b d)"), bank[5][:, :], xb[:, :], ALU.add)\
                    .then_inc(ff.res_sum, 1)
                dve.drain()
                norm_stats(dve, ff, res, NB)
                dve.wait_ge(ff.rstd, done(n, 2, 1))
                normalize(dve, ff, nrm, res, NB)
                dve.wait_ge(ff.affine, done(n, 1, 1))
                nc.vector.tensor_tensor(ff_sum.rearrange("p b d -> p (b d)"), nrm[:].rearrange("p b d -> p (b d)"),
                                        X4[:, n, :], ALU.add)
                dve.drain()
                norm_stats(dve, ff, ff_sum, NB)
                dve.wait_ge(ff.rstd, done(n, 2, 2))
                normalize(dve, ff, by4(X4[:, n, :]), ff_sum, NB)
                dve.drain()

        def ffn_pool(pool):
            def body(n):
                pool.drain()
                pool.wait_ge(ff.stats, done(n, 2, 0))
                carry_wait(pool)
                nc.gpsimd.tensor_tensor(by4(xb[:, :]), by4(H4[:, n, :]), row4("fc2_b"), ALU.add)\
                    .then_inc(ff.xb_sb, 1)
                pool.wait_ge(ff.stats, done(n, 2, 1))
                inv_std(pool, ff, NB, lneps[:, 0:NB], mv[:, 0:NB, 1])
                pool.wait_ge(ff.normed, done(n, 2, 1))
                nc.gpsimd.tensor_tensor(nrm[:], nrm[:], row4("ln3_g"), ALU.mult)
                pool.drain()
                nc.gpsimd.tensor_tensor(nrm[:], nrm[:], row4("ln3_b"), ALU.add).then_inc(ff.affine, 1)
                pool.wait_ge(ff.stats, done(n, 2, 2))
                inv_std(pool, ff, NB, lneps[:, 0:NB], mv[:, 0:NB, 1])
            fetching(pool, lambda n: fetch(pool, ff, [(xs, H4[:, n, :])], ff.xT_ready, done(n, 1, 0)), body)

        r = Room()
        g0_t = [r.take(W) for _ in range(2)]
        g0_sq = r.take(NB)
        g0_logits = r.take(B, E0)
        g0_best = r.take(2, B)
        g0_eq = r.take(B, E0)
        g0_hot = [r.take(B, E0) for _ in range(2)]
        g0_top = r.take(B)
        g0_rest = r.take(B, E0)
        g0_gap = r.take(B)
        g0_w = r.take(2, B)
        combine0 = r.take(B, E0)
        ROUTER0 = r.at

        def spread(ap, n=8):
            return ap.unsqueeze(2).to_broadcast([128, B, n])

        def top_two(dve, logits, best, eq, hot, top, rest):
            order = rank[:, :].unsqueeze(1).to_broadcast([128, B, 8])
            src = logits
            for k in range(2):
                nc.vector.tensor_reduce(best[:, k, :], src, AX.X, ALU.max)
                dve.drain()
                nc.vector.tensor_tensor(eq, src, spread(best[:, k, :]), ALU.is_equal)
                dve.drain()
                nc.vector.tensor_tensor(eq, eq, order, ALU.mult)
                dve.drain()
                nc.vector.tensor_reduce(top, eq, AX.X, ALU.max)
                dve.drain()
                nc.vector.tensor_tensor(hot[k], order, spread(top), ALU.is_equal)
                dve.drain()
                if k == 0:
                    nc.vector.scalar_tensor_tensor(rest.rearrange("p b e -> p (b e)"),
                                                   hot[0].rearrange("p b e -> p (b e)"), -3e38,
                                                   src.rearrange("p b e -> p (b e)"), ALU.mult, ALU.add)
                    dve.drain()
                    src = rest

        def router0_dve(dve):
            with dve.Fori(0, NIT) as n:
                norm_src = by4(X4[:, n, :])
                for b in range(NB):
                    nc.vector.tensor_copy(nrm[:, b, :], norm_src[:, b, :])
                dve.drain()
                for b in range(NB):
                    nc.vector.bn_stats(stats[:, b, :], nrm[:, b, :])
                dve.drain()
                for b in range(NB):
                    nc.vector.bn_aggr(mv[:, b, :], stats[:, b, :])
                dve.drain()
                nc.vector.tensor_tensor(g0_sq, mv[:, 0:NB, 0], mv[:, 0:NB, 0], ALU.mult)
                dve.drain()
                nc.vector.tensor_tensor(g0_sq, g0_sq, mv[:, 0:NB, 1], ALU.add).then_inc(g0.stats, 1)
                dve.wait_ge(g0.rstd, done(n, 1, 1))
                dve.wait_ge(g0.tT_ready, done(n, 1, 0))
                for b in range(NB):
                    last = nc.vector.scalar_tensor_tensor(g0_t[0][:, b * D:(b + 1) * D], nrm[:, b, :],
                                                          rstd[:, b:b + 1], rows["norm_w"][:, :], ALU.mult, ALU.mult)
                last.then_inc(g0.tokens, 1)
                dve.drain()
            dve.wait_ge(g0.logits_sb, done(NIT, 1, 0))
            top_two(dve, g0_logits, g0_best, g0_eq, g0_hot, g0_top, g0_rest)
            nc.vector.tensor_tensor(g0_gap, g0_best[:, 1, :], g0_best[:, 0, :], ALU.subtract)\
                .then_inc(g0.gap, 1)
            dve.wait_ge(g0.gap_exp, PRIME + 1)
            nc.vector.tensor_scalar(g0_w[:, 0, :], g0_gap, 1.0, None, ALU.add)
            dve.drain()
            nc.vector.reciprocal(g0_w[:, 0, :], g0_w[:, 0, :])
            dve.drain()
            nc.vector.tensor_tensor(g0_w[:, 1, :], g0_w[:, 0, :], g0_gap, ALU.mult)
            dve.drain()
            for k in range(2):
                nc.vector.tensor_tensor(g0_hot[k], g0_hot[k], spread(g0_w[:, k, :]), ALU.mult)
            dve.drain()
            nc.vector.tensor_tensor(combine0, g0_hot[0], g0_hot[1], ALU.add).then_inc(g0.combine, 1)

        def router0_pool(pool):
            with pool.Fori(0, NIT) as n:
                pool.wait_ge(g0.stats, done(n, 1, 1))
                inv_std(pool, g0, NB, rmseps[:, 0:NB], g0_sq)

        def router0_pe(pe):
            with pe.Fori(0, NIT) as n:
                pe.wait_ge(g0.tokens, done(n, 1, 1))
                pe.wait_ge(g0.tT_sb, done(n, 1, 0))
                for b in range(NB):
                    last = nc.tensor.transpose(bank[0][:, b * T:(b + 1) * T], g0_t[0][:, b * D:(b + 1) * D], ident[:])
                last.then_inc(g0.tT_ready, 1)
                pe.wait_ge(g0.tT_sb, done(n, 1, 1))
                pe.wait_ge(g0.logits_sb, done(n, 1, 0))
                for b in range(NB):
                    last = nc.tensor.matmul(bank[1][:, b * E0:(b + 1) * E0], g0_t[1][:, b * T:(b + 1) * T],
                                            gate0[:, :], start=True, stop=True)
                last.then_inc(g0.logits, 1)

        def router0_act(act):
            L4 = g0_logits.rearrange("p (i b) e -> p i (b e)", b=NB)
            with act.Fori(0, NIT) as n:
                act.wait_ge(g0.tT_ready, done(n, 1, 1))
                nc.scalar.activation(g0_t[1], bank[0][:, :], ACT.Copy)
                act.drain()
                nc.scalar.activation(H4[:, n, :], g0_t[1], ACT.Copy).then_inc(g0.tT_sb, 1)
                act.drain()
                act.wait_ge(g0.logits, done(n, 1, 1))
                carry_wait(act)
                nc.scalar.activation(L4[:, n, :], bank[1][:, 0:NB * E0], ACT.Copy).then_inc(g0.logits_sb, 1)
            act.wait_ge(g0.gap, PRIME + 1)
            nc.scalar.activation(g0_gap, g0_gap, ACT.Exp).then_inc(g0.gap_exp, 1)

        r = Room()
        r.at = ROUTER0
        m0_tT = r.take(W)
        m0_c = r.take(NB, E0)
        m0_cT = r.take(W, parts=E0)
        m0_h = [r.take(HID // 128, W) for _ in range(2)]
        NH0 = HID // 128

        def moe0_pe(pe):
            with pe.Fori(0, NIT) as n:
                pe.wait_ge(m0.xT_sb, done(n, 2, 1))
                pe.wait_ge(m0.acc, done(n, E0 + 1, 0))
                for b in range(NB):
                    last = nc.tensor.transpose(bank[6][0:E0, b * T:(b + 1) * T], m0_c[:, b, :], ident[:])
                last.then_inc(m0.xT_ready, 1)
                pe.wait_ge(m0.xT_sb, done(n, 2, 2))
                for b in range(NB):
                    last = nc.tensor.matmul(bank[7][:, b * D:(b + 1) * D], m0_cT[:, b * T:(b + 1) * T], b2_sb[:, :],
                                            start=True, stop=True)
                last.then_inc(m0.bias, 1)
                for e in range(E0 + 1):
                    if e < E0:
                        for t in range(NH0):
                            k = e * NH0 + t
                            if k >= 4:
                                pe.wait_ge(m0.gelu, done(n, E0 * NH0, k - 3))
                            nc.tensor.matmul(bank[k % 4][:], w1_l0[:, e, t * 128:(t + 1) * 128], m0_tT[:, :],
                                             start=True, stop=True).then_inc(m0.up, 1)
                    if e >= 1:
                        f = e - 1
                        pe.wait_ge(m0.gelu, done(n, E0 * NH0, (f + 1) * NH0))
                        if f >= 2:
                            pe.wait_ge(m0.acc, done(n, E0 + 1, f))
                        for b in range(NB):
                            for t in range(NH0):
                                last = nc.tensor.matmul(bank[4 + f % 2][:, b * D:(b + 1) * D],
                                                        m0_h[f % 2][:, t, b * T:(b + 1) * T], w2_l0[:, f, t, :],
                                                        start=(t == 0), stop=(t == NH0 - 1))
                        last.then_inc(m0.down, 1)

        def moe0_act(act):
            c4 = combine0.rearrange("p (i b) e -> p i (b e)", b=NB)
            with act.Fori(0, NIT) as n:
                act.drain()
                act.wait_ge(m0.down, done(n, E0, 0))
                carry_wait(act)
                act.drain()
                act.wait_ge(m0.acc, done(n, E0 + 1, 0))
                carry_wait(act)
                nc.scalar.activation(m0_tT[:, :], H4[:, n, :], ACT.Copy)
                nc.scalar.activation(m0_c.rearrange("p b e -> p (b e)"), c4[:, n, :], ACT.Copy)\
                    .then_inc(m0.xT_sb, 1)
                act.wait_ge(m0.xT_ready, done(n, 1, 1))
                nc.scalar.activation(m0_cT[:, :], bank[6][0:E0, :], ACT.Copy).then_inc(m0.xT_sb, 1)
                for k in range(E0 * NH0):
                    e, t = k // NH0, k % NH0
                    act.wait_ge(m0.up, done(n, E0 * NH0, k + 1))
                    if t == 0 and e >= 2:
                        act.wait_ge(m0.down, done(n, E0, e - 1))
                    nc.scalar.activation(m0_h[e % 2][:, t, :], bank[k % 4][:, :], ACT.Gelu,
                                         bias=cols["b1"][:, k:k + 1]).then_inc(m0.gelu, 1)

        def moe0_dve(dve):
            with dve.Fori(0, NIT) as n:
                dve.wait_ge(m0.bias, done(n, 1, 1))
                nc.vector.scalar_tensor_tensor(res[:].rearrange("p b d -> p (b d)"), X4[:, n, :], 2.0,
                                               bank[7][:, :], ALU.mult, ALU.add).then_inc(m0.acc, 1)
                dve.drain()
                for e in range(E0):
                    dve.wait_ge(m0.down, done(n, E0, e + 1))
                    for b in range(NB):
                        last = nc.vector.scalar_tensor_tensor(res[:, b, :], bank[4 + e % 2][:, b * D:(b + 1) * D],
                                                              m0_c[:, b, e:e + 1], res[:, b, :], ALU.mult, ALU.add)
                    last.then_inc(m0.acc, 1)
                    dve.drain()
                norm_stats(dve, m0, res, NB)
                dve.wait_ge(m0.rstd, done(n, 1, 1))
                normalize(dve, m0, by4(X4[:, n, :]), res, NB)
                dve.drain()

        def moe0_pool(pool):
            with pool.Fori(0, NIT) as n:
                pool.wait_ge(m0.stats, done(n, 1, 1))
                inv_std(pool, m0, NB, lneps[:, 0:NB], mv[:, 0:NB, 1])

        r = Room()
        l1_xT = r.take(W)
        l1_qk = r.take(NB, 2 * D)
        l1_c = r.take(NB, 2 * D)
        l1_s = r.take(NB, 2 * D)
        l1_rot = r.take(NB, 2 * D)
        l1_q = [r.take(W) for _ in range(2)]
        l1_k = [r.take(W) for _ in range(2)]
        l1_v = [r.take(NB, HEADS, DH1 + 1) for _ in range(2)]
        l1_kblk = [r.take(HEADS, T) for _ in range(2)]
        l1_probs = [r.take(GH, T) for _ in range(2)]
        l1_probsT = [r.take(GH, T) for _ in range(2)]
        l1_heads = [r.take(D)] * 2
        l1_headsT = r.take(1, 128)
        l1_nmax = r.take(4, GH)
        l1_recip = r.take(2, GH)
        OUT1 = NB * 2
        NPROJ1 = 1 + NB + 2
        QKV = 3 * D

        def pairs(eng, first, body):
            first()
            body(0, 0, False, True)
            with eng.Fori(0, (NIT - 2) // 2) as i:
                body(i * 2 + 1, 1, True, True)
                body(i * 2 + 2, 0, True, True)
            body(NIT - 1, 1, True, False)

        STATS_STEP, NORM_STEP = 0, 3

        PROJ_STEPS = [0, 1, 2, 3, 4, 10, 11]

        def proj1_pe(pe, n, k):
            if k > NB:
                pe.wait_ge(l1.roped, done(n, 1, 1))
            pe.wait_ge(l1.proj_used, done(n, NPROJ1, k))
            o = bank[6]
            if k == 0:
                pe.wait_ge(l1.fetched, done(n, 1, 1))
            if k == 0:
                for b in range(NB):
                    last = nc.tensor.transpose(o[:, b * T:(b + 1) * T], xs[:, b * D:(b + 1) * D], ident[:])
            elif k <= NB:
                b = k - 1
                last = nc.tensor.matmul(o[:, 0:QKV], l1_xT[:, b * T:(b + 1) * T], w_l1[:, 0:QKV],
                                        start=True, stop=True)
            else:
                j = k - NB - 1
                for b in range(NB):
                    last = nc.tensor.transpose(o[:, b * T:(b + 1) * T], l1_rot[:, b, j * D:(j + 1) * D], ident[:])
            last.then_inc(l1.proj_ready, 1)

        def proj1_dve(dve, n, s, k):
            o = bank[6]
            if k == 1:
                dve.wait_ge(l1.roped, done(n, 1, 0))
            dve.wait_ge(l1.proj_ready, done(n, NPROJ1, k + 1))
            if k == 0:
                last = nc.vector.tensor_copy(l1_xT[:, :], o[:, :])
            elif k <= NB:
                b = k - 1
                nc.vector.tensor_tensor(l1_qk[:, b, :], o[:, 0:2 * D], rows["l1_bqkv"][:, 0:2 * D], ALU.add)
                last = nc.vector.tensor_tensor(l1_v[s][:, b, :, 0:DH1],
                                               o[:, 2 * D:3 * D].rearrange("p (h d) -> p h d", d=DH1),
                                               rows["l1_bqkv"][:, 2 * D:3 * D].rearrange("p (h d) -> p h d", d=DH1),
                                               ALU.add)
            elif k == NB + 1:
                last = nc.vector.tensor_scalar(l1_q[s][:, :], o[:, :], DH1 ** -0.5, None, ALU.mult)
            else:
                last = nc.vector.tensor_copy(l1_k[s][:, :], o[:, :])
            last.then_inc(l1.proj_used, 1)

        class OutRing1:

            def __init__(self, pe, stage, per):
                self.pe, self.stage, self.per, self.count = pe, stage, per, 0

            def __call__(self, n):
                self.pe.wait_ge(self.stage.out_used, done(n, self.per, self.count))
                self.count += 1
                return bank[7]

        def attn1_pe(pe):
            def body(n, s, behind, ahead):
                def scores(g):
                    b = g // GB
                    if g % GB == 0:
                        pe.wait_ge(l1.kblk, done(n, NB, b + 1))
                    nc.tensor.matmul(bank[S_BANK + g % 2][:], l1_q[s][:, b * T:(b + 1) * T],
                                     l1_kblk[b % 2][:, (g % GB) * GH:(g % GB + 1) * GH, :]
                                     .rearrange("p h t -> p (h t)"), start=True, stop=True)\
                        .then_inc(l1.scores, 1)

                def hook(step):
                    if ahead and step in PROJ_STEPS:
                        proj1_pe(pe, n + 1, PROJ_STEPS.index(step))
                softmax_pe(pe, l1, n, scores, l1_v[s], l1_probs, l1_probsT, l1_heads, l1_headsT,
                           w_l1[:, QKV:QKV + D], DH1, OutRing1(pe, l1, OUT1), hook)

            def first():
                for k in range(NPROJ1):
                    proj1_pe(pe, 0, k)
            pairs(pe, first, body)

        def attn1_act(act):
            with act.Fori(0, NIT) as n:
                softmax_act(act, l1, n, l1_nmax, l1_probs, l1_probsT)

        def attn1_dve(dve):
            def body(n, s, behind, ahead):
                def hook(step):
                    if ahead and step - 1 in PROJ_STEPS:
                        proj1_dve(dve, n + 1, 1 - s, PROJ_STEPS.index(step - 1))
                    if behind and step == STATS_STEP:
                        norm_stats(dve, l1, res, NB)
                    if behind and step == NORM_STEP:
                        norm1(n - 1)
                softmax1_dve(dve, l1, n, l1_nmax, l1_recip, l1_heads, l1_headsT, hook)

            def norm1(n):
                dve.wait_ge(l1.rstd, done(n, 1, 1))
                normalize(dve, l1, by4(X4[:, n, :]), res, NB)
                dve.drain()

            def first():
                for k in range(NPROJ1):
                    proj1_dve(dve, 0, 0, k)
            pairs(dve, first, body)
            norm_stats(dve, l1, res, NB)
            norm1(NIT - 1)

        def softmax1_dve(dve, stage, n, nmax, recip, heads, headsT, hook):
            used = 0
            for step, g_s, g_t, g_v, b_ot, b_wo in steps():
                if g_s is not None:
                    dve.wait_ge(stage.scores, done(n, NG, g_s + 1))
                    nc.vector.tensor_reduce(nmax[:, g_s % 4, :],
                                            bank[S_BANK + g_s % 2][:, :].rearrange("p (h t) -> p h t", h=GH),
                                            AX.X, ALU.max, negate=True).then_inc(stage.maxes, 1)
                hook(step)
                if g_v is not None:
                    dve.wait_ge(stage.pv, done(n, NG, g_v + 1))
                    if g_v % GB == 0:
                        b = g_v // GB
                        dve.wait_ge(stage.out_ready, done(n, OUT1, b * 2 - 1 if b else 0))
                    o = bank[O_BANK + g_v % 2][:, 0:GH * (DH1 + 1)].rearrange("p (h d) -> p h d", h=GH)
                    nc.vector.reciprocal(recip[:, g_v % 2, :], o[:, :, DH1])
                    dve.drain()
                    q = g_v % GB
                    nc.vector.tensor_tensor(
                        heads[0][:, q * GH * DH1:(q + 1) * GH * DH1].rearrange("p (h d) -> p h d", h=GH),
                        o[:, :, 0:DH1], recip[:, g_v % 2, :].unsqueeze(2).to_broadcast([128, GH, DH1]), ALU.mult)\
                        .then_inc(stage.heads_sb, 1)
                if b_ot is not None:
                    dve.wait_ge(stage.out_ready, done(n, OUT1, used + 1))
                    nc.vector.tensor_copy(headsT[:, 0, :], bank[7][:, 0:128]).then_inc(stage.out_used, 1)
                    used += 1
                if b_wo is not None:
                    dve.wait_ge(stage.out_ready, done(n, OUT1, used + 1))
                    if b_wo == 0:
                        dve.wait_ge(stage.xb_sb, done(n, 1, 1))
                    nc.vector.tensor_tensor(res[:, b_wo, :], bank[7][:, 0:D], xb[:, b_wo * D:(b_wo + 1) * D],
                                            ALU.add).then_inc(stage.out_used, 1)
                    used += 1
            dve.drain()

        def attn1_pool(pool):
            def rope(n):
                pool.wait_ge(l1.proj_used, done(n, NPROJ1, 1 + NB))
                pool.wait_ge(l1.proj_ready, done(n, NPROJ1, 0))
                qk = l1_qk.rearrange("p b (h d) -> p (b h) d", d=DH1)
                nh = NB * 2 * HEADS
                c, s, o = (t.rearrange("p b (h d) -> p (b h) d", d=DH1) for t in (l1_c, l1_s, l1_rot))
                nc.gpsimd.tensor_tensor(c, qk, cosr[:, :].unsqueeze(1).to_broadcast([128, nh, DH1]), ALU.mult)
                nc.gpsimd.tensor_tensor(s, qk, sinr[:, :].unsqueeze(1).to_broadcast([128, nh, DH1]), ALU.mult)
                pool.drain()
                m = DH1 // 2
                nc.gpsimd.tensor_tensor(o[:, :, 0:m], c[:, :, 0:m], s[:, :, m:DH1], ALU.subtract)
                nc.gpsimd.tensor_tensor(o[:, :, m:DH1], c[:, :, m:DH1], s[:, :, 0:m], ALU.add)\
                    .then_inc(l1.roped, 1)
                pool.drain()

            def kblk(n, s, b, free):
                if b == 0:
                    pool.wait_ge(l1.proj_used, done(n, NPROJ1, NPROJ1))
                pool.wait_ge(l1.scores, free)
                nc.gpsimd.tensor_tensor(l1_kblk[b % 2],
                                        l1_k[s][:, b * T:(b + 1) * T].unsqueeze(1).to_broadcast([128, HEADS, T]),
                                        headmask[:, :].unsqueeze(2).to_broadcast([128, HEADS, T]), ALU.mult)\
                    .then_inc(l1.kblk, 1)

            def body(n, s, behind, ahead):
                if ahead:
                    fetch1(n + 1)
                kblk(n, s, 1, done(n, NG, 0))
                pool.drain()
                pool.wait_ge(l1.stats, done(n, 1, 0))
                carry_wait(pool)
                if behind:
                    inv_std(pool, l1, NB, lneps[:, 0:NB], mv[:, 0:NB, 1])
                nc.gpsimd.tensor_tensor(by4(xb[:, :]), by4(X4[:, n, :]), row4("l1_bo"), ALU.add)\
                    .then_inc(l1.xb_sb, 1)
                kblk(n, s, 2, done(n, NG, GB))
                if ahead:
                    rope(n + 1)
                kblk(n, s, 3, done(n, NG, 2 * GB))
                if ahead:
                    kblk(n + 1, 1 - s, 0, done(n, NG, 3 * GB))

            def fetch1(n):
                fetch(pool, l1, [(xs, X4[:, n, :])], l1.proj_ready, done(n, NPROJ1, 1 - NPROJ1))

            def first():
                fetch1(0)
                rope(0)
                kblk(0, 0, 0, done(0, NG, 0))

            pairs(pool, first, body)
            pool.wait_ge(l1.stats, done(NIT, 1, 0))
            inv_std(pool, l1, NB, lneps[:, 0:NB], mv[:, 0:NB, 1])

        r = Room()
        lx_xT = r.take(W)
        lx_cT = r.take(W)
        lx_mi = [r.take(NB, T).bitcast(mybir.dt.int32) for _ in range(2)]
        lx_mf = r.take(NB, T)
        lx_mT = [r.take(NB, T) for _ in range(2)]
        lx_q = [r.take(W) for _ in range(2)]
        lx_k = [r.take(W) for _ in range(2)]
        lx_v = [r.take(NB, D) for _ in range(2)]
        lx_qblk = [r.take(HEADS, T) for _ in range(2)]
        lx_w = [r.take(GH, T) for _ in range(3)]
        lx_heads = r.take(D)
        lx_headsT = r.take(D)
        NPROJX = 6

        def projx_pe(pe, n, k):
            if k == 2:
                pe.wait_ge(lx.mask_f, done(n, 1, 1))
            pe.wait_ge(lx.proj_used, done(n, NPROJX, k))
            o = bank[6]
            if k == 0:
                pe.wait_ge(lx.fetched, done(n, 1, 1))
            if k < 2:
                for b in range(NB):
                    last = nc.tensor.transpose(o[:, b * T:(b + 1) * T], (xs, cs)[k][:, b * D:(b + 1) * D], ident[:])
            elif k == 2:
                for b in range(NB):
                    last = nc.tensor.transpose(o[:, b * T:(b + 1) * T], lx_mf[:, b, :], ident[:])
            elif k < 5:
                last = nc.tensor.matmul(o[:], w_l1x[:, k - 3, :], (lx_xT, lx_cT)[k - 3][:, :], start=True, stop=True)
            else:
                for b in range(NB):
                    last = nc.tensor.matmul(o[:, b * D:(b + 1) * D], lx_cT[:, b * T:(b + 1) * T], w_l1x[:, 2, :],
                                            start=True, stop=True)
            last.then_inc(lx.proj_ready, 1)

        def projx_act(act, n, s, k):
            dst = (lx_xT[:, :], lx_cT[:, :], lx_mT[s].rearrange("p b t -> p (b t)"), lx_q[s][:, :], lx_k[s][:, :],
                   lx_v[s].rearrange("p b d -> p (b d)"))[k]
            act.wait_ge(lx.proj_ready, done(n, NPROJX, k + 1))
            if k in (3, 4):
                bias = cols[("l1x_bq", "l1x_bk")[k - 3]]
                last = nc.scalar.activation(dst, bank[6][:, :], ACT.Identity, bias=bias[:, 0:1])
            else:
                last = nc.scalar.activation(dst, bank[6][:, :], ACT.Copy)
            last.then_inc(lx.proj_used, 1)

        def allx(f):
            for k in range(NPROJX):
                f(k)

        def stepsx():
            for n in range(-1, NG + 4):
                ot = (n - GB - 1) // GB if (n - GB - 1) % GB == 0 and n > GB else None
                wo = (n - GB - 2) // GB if (n - GB - 2) % GB == 0 and n > GB + 1 else None
                yield n, (n + 1 if n + 1 < NG else None), (n - 1 if 1 <= n <= NG else None), ot, wo

        PROJ_X = list(range(3, 3 + NPROJX))

        def attnx_pe(pe):
            def body(n, s, behind, ahead):
                used = 0
                for step, g_s, g_v, b_ot, b_wo in stepsx():
                    if g_s is not None:
                        b = g_s // GB
                        if g_s % GB == 0:
                            pe.wait_ge(lx.qblk, done(n, NB, b + 1))
                        pe.wait_ge(lx.silu, done(n, NG, g_s - 1))
                        nc.tensor.matmul(bank[S_BANK + g_s % 2][:], lx_k[s][:, b * T:(b + 1) * T],
                                         lx_qblk[b % 2][:, (g_s % GB) * GH:(g_s % GB + 1) * GH, :]
                                         .rearrange("p h t -> p (h t)"), start=True, stop=True)\
                            .then_inc(lx.scores, 1)
                    if g_v is not None:
                        b = g_v // GB
                        pe.wait_ge(lx.masked, done(n, NG, g_v + 1))
                        if g_v % GB == 0:
                            pe.wait_ge(lx.heads_sb, done(n, 2 * NB, 2 * b - 2))
                        for h in range(GH):
                            head = (g_v % GB) * GH + h
                            last = nc.tensor.matmul(bank[O_BANK + b % 2][:, head * DH1:(head + 1) * DH1],
                                                    lx_w[g_v % 3][:, h, :],
                                                    lx_v[s][:, b, head * DH1:(head + 1) * DH1], start=True, stop=True)
                        last.then_inc(lx.pv, 1)
                    if b_ot is not None:
                        pe.wait_ge(lx.heads_sb, done(n, 2 * NB, 2 * b_ot + 1))
                        pe.wait_ge(lx.out_used, done(n, NB, b_ot))
                        nc.tensor.transpose(bank[7][:, 0:128], lx_heads[:, :], ident[:])\
                            .then_inc(lx.out_ready, 1)
                    if b_wo is not None:
                        pe.wait_ge(lx.heads_sb, done(n, 2 * NB, 2 * b_wo + 2))
                        nc.tensor.matmul(bank[7][:, 0:D], lx_headsT[:, :], w_l1x[:, 3, :], start=True, stop=True)\
                            .then_inc(lx.out_ready, 1)
                    if ahead and step in PROJ_X:
                        projx_pe(pe, n + 1, PROJ_X.index(step))
            pairs(pe, lambda: allx(lambda k: projx_pe(pe, 0, k)), body)

        def attnx_act(act):
            def body(n, s, behind, ahead):
                for step, g_s, g_v, b_ot, b_wo in stepsx():
                    if g_s is not None:
                        act.wait_ge(lx.scores, done(n, NG, g_s + 1))
                        if g_s >= 3:
                            act.wait_ge(lx.pv, done(n, NG, g_s - 2))
                        else:
                            act.wait_ge(lx.pv, done(n, NG, 0))
                        nc.scalar.activation(lx_w[g_s % 3].rearrange("p h t -> p (h t)"), bank[S_BANK + g_s % 2][:, :],
                                             ACT.Silu, scale=DH1 ** -0.5).then_inc(lx.silu, 1)
                    if ahead and step - 1 in PROJ_X:
                        projx_act(act, n + 1, 1 - s, PROJ_X.index(step - 1))
                    if b_ot is not None:
                        act.wait_ge(lx.pv, done(n, NG, (b_ot + 1) * GB))
                        act.wait_ge(lx.out_ready, done(n, 2 * NB, 2 * b_ot - 1 if b_ot else 0))
                        nc.scalar.activation(lx_heads[:, :], bank[O_BANK + b_ot % 2][:, 0:D], ACT.Copy)\
                            .then_inc(lx.heads_sb, 1)
                        act.wait_ge(lx.out_ready, done(n, 2 * NB, 2 * b_ot + 1))
                        nc.scalar.activation(lx_headsT[:, :], bank[7][:, 0:128], ACT.Copy)\
                            .then_inc(lx.heads_sb, 1)
            pairs(act, lambda: allx(lambda k: projx_act(act, 0, 0, k)), body)

        def attnx_dve(dve):
            def mask(n, s):
                dve.wait_ge((lx.mask_in_even, lx.mask_in_odd)[s], done(n, 8, 16 - 8 * s))
                dve.wait_ge(lx.proj_ready, done(n, NPROJX, 0))
                nc.vector.tensor_scalar(lx_mf, lx_mi[s], 0, None, ALU.not_equal).then_inc(lx.mask_f, 1)

            def v_bias(n, s):
                dve.wait_ge(lx.proj_used, done(n, NPROJX, NPROJX))
                nc.vector.tensor_tensor(lx_v[s], lx_v[s], row4("l1x_bv"), ALU.add)
                dve.drain()

            def body(n, s, behind, ahead):
                for step, g_s, g_v, b_ot, b_wo in stepsx():
                    if g_s is not None:
                        dve.wait_ge(lx.silu, done(n, NG, g_s + 1))
                        nc.vector.tensor_tensor(lx_w[g_s % 3], lx_w[g_s % 3],
                                                lx_mT[s][:, g_s // GB, :].unsqueeze(1).to_broadcast([128, GH, T]),
                                                ALU.mult).then_inc(lx.masked, 1)
                    if b_wo is not None:
                        dve.wait_ge(lx.out_ready, done(n, 2 * NB, 2 * b_wo + 2))
                        nc.vector.tensor_tensor(res[:, b_wo, :], bank[7][:, 0:D],
                                                X4[:, n, b_wo * D:(b_wo + 1) * D], ALU.add)\
                            .then_inc(lx.out_used, 1)
                    if ahead and step == PROJ_X[-1] + 2:
                        v_bias(n + 1, 1 - s)
                    if behind and step == STATS_STEP:
                        norm_stats(dve, lx, res, NB)
                    if ahead and step == 1:
                        mask(n + 1, 1 - s)
                    if behind and step == NORM_STEP:
                        normx(n - 1)
                dve.drain()

            def normx(n):
                dve.wait_ge(lx.rstd, done(n, 1, 1))
                normalize(dve, lx, by4(X4[:, n, :]), res, NB)
                dve.drain()

            def first():
                mask(0, 0)
                v_bias(0, 0)
            pairs(dve, first, body)
            norm_stats(dve, lx, res, NB)
            normx(NIT - 1)

        def attnx_pool(pool):
            def qblk(n, s, b, free):
                if b == 0:
                    pool.wait_ge(lx.proj_used, done(n, NPROJX, NPROJX))
                pool.wait_ge(lx.scores, free)
                nc.gpsimd.tensor_tensor(lx_qblk[b % 2],
                                        lx_q[s][:, b * T:(b + 1) * T].unsqueeze(1).to_broadcast([128, HEADS, T]),
                                        headmask[:, :].unsqueeze(2).to_broadcast([128, HEADS, T]), ALU.mult)\
                    .then_inc(lx.qblk, 1)

            def fetchx(n):
                fetch(pool, lx, [(xs, X4[:, n, :]), (cs, C4[:, n, :])], lx.proj_ready, done(n, NPROJX, 2 - NPROJX))

            def first():
                fetchx(0)
                qblk(0, 0, 0, done(0, NG, 0))

            def body(n, s, behind, ahead):
                qblk(n, s, 1, done(n, NG, 0))
                if behind:
                    pool.wait_ge(lx.stats, done(n, 1, 0))
                    inv_std(pool, lx, NB, lneps[:, 0:NB], mv[:, 0:NB, 1])
                if ahead:
                    fetchx(n + 1)
                for b in range(2, NB):
                    qblk(n, s, b, done(n, NG, (b - 1) * GB))
                if ahead:
                    qblk(n + 1, 1 - s, 0, done(n, NG, 3 * GB))
            pairs(pool, first, body)
            pool.wait_ge(lx.stats, done(NIT, 1, 0))
            inv_std(pool, lx, NB, lneps[:, 0:NB], mv[:, 0:NB, 1])

        def attnx_sp(sp, mask_dram):
            def load(n, s):
                sp.dma_start(lx_mi[s], mask_dram[n]).then_inc((lx.mask_in_even, lx.mask_in_odd)[s], 16)
            load(0, 0)
            load(1, 1)
            with sp.Fori(0, (NIT - 2) // 2) as i:
                for j in (0, 1):
                    n = i * 2 + (j + 2)
                    sp.wait_ge(lx.mask_f, done(n, 1, -1))
                    load(n, j)

        r = Room()
        g1_xT = r.take(W)
        g1_logits = r.take(B, E1)
        g1_best = r.take(2, B)
        g1_eq = r.take(B, E1)
        g1_hot = [r.take(B, E1) for _ in range(2)]
        g1_top = r.take(B)
        g1_rest = r.take(B, E1)
        g1_max = r.take(B)
        g1_sum = r.take(B)
        g1_chosen = r.take(B * E1 // 2).bitcast(BF16)
        probs1 = r.take(B, E1)
        place1 = r.take(B, E1)
        ROUTER1 = r.at

        def router1_pe(pe):
            with pe.Fori(0, NIT) as n:
                pe.wait_ge(g1.xT_sb, done(n, 1, 0))
                pe.wait_ge(g1.fetched, done(n, 1, 1))
                for b in range(NB):
                    last = nc.tensor.transpose(bank[0][:, b * T:(b + 1) * T], xs[:, b * D:(b + 1) * D], ident[:])
                last.then_inc(g1.xT_ready, 1)
                pe.wait_ge(g1.xT_sb, done(n, 1, 1))
                pe.wait_ge(g1.logits_sb, done(n, 1, 0))
                for b in range(NB):
                    last = nc.tensor.matmul(bank[1][:, b * E1:(b + 1) * E1], g1_xT[:, b * T:(b + 1) * T],
                                            gate1[:, :], start=True, stop=True)
                last.then_inc(g1.logits, 1)
            pe.wait_ge(g1.chosen, PRIME + 1)
            nc.tensor.matmul(bank[2][:, 0:B * E1], upper[:, :], g1_chosen[:, :], start=True, stop=True)\
                .then_inc(g1.counts, 1)

        def router1_pool(pool):
            fetching(pool, lambda n: fetch(pool, g1, [(xs, X4[:, n, :])], g1.xT_ready, done(n, 1, 0)),
                     lambda n: None)

        def router1_act(act):
            L4 = g1_logits.rearrange("p (i b) e -> p i (b e)", b=NB)
            with act.Fori(0, NIT) as n:
                act.wait_ge(g1.xT_ready, done(n, 1, 1))
                nc.scalar.activation(g1_xT, bank[0][:, :], ACT.Copy).then_inc(g1.xT_sb, 1)
                act.drain()
                act.wait_ge(g1.logits, done(n, 1, 1))
                carry_wait(act)
                nc.scalar.activation(L4[:, n, :], bank[1][:, 0:NB * E1], ACT.Copy).then_inc(g1.logits_sb, 1)
            act.wait_ge(g1.shifted, PRIME + 1)
            nc.scalar.activation(probs1, g1_logits, ACT.Exp).then_inc(g1.exps, 1)

        def router1_dve(dve):
            dve.wait_ge(g1.logits_sb, done(NIT, 1, 0))
            nc.vector.tensor_reduce(g1_max, g1_logits, AX.X, ALU.max)
            dve.drain()
            nc.vector.tensor_tensor(g1_logits, g1_logits, spread(g1_max), ALU.subtract)\
                .then_inc(g1.shifted, 1)
            dve.wait_ge(g1.exps, PRIME + 1)
            nc.vector.tensor_reduce(g1_sum, probs1, AX.X, ALU.add)
            dve.drain()
            nc.vector.reciprocal(g1_sum, g1_sum)
            dve.drain()
            nc.vector.tensor_tensor(probs1, probs1, spread(g1_sum), ALU.mult)
            dve.drain()
            top_two(dve, probs1, g1_best, g1_eq, g1_hot, g1_top, g1_rest)
            nc.vector.tensor_tensor(g1_eq, g1_hot[0], g1_hot[1], ALU.add)
            dve.drain()
            nc.vector.tensor_copy(g1_chosen, g1_eq.rearrange("p b e -> p (b e)")).then_inc(g1.chosen, 1)
            dve.wait_ge(g1.counts, PRIME + 1)
            nc.vector.tensor_tensor(g1_rest.rearrange("p b e -> p (b e)"), bank[2][:, 0:B * E1],
                                    g1_eq.rearrange("p b e -> p (b e)"), ALU.mult)
            dve.drain()
            nc.vector.tensor_copy(place1, g1_rest).then_inc(g1.places, 1)

        r = Room()
        r.at = ROUTER1
        m1_hot = [r.take(E1, CAP) for _ in range(2)]
        m1_comb = [r.take(EC) for _ in range(2)]
        m1_p = r.take(NB1, E1)
        m1_pl = r.take(NB1, E1)
        m1_disp = r.take(E1, NB1, CAP)
        m1_combT = r.take(NB1, 3, T)
        m1_s = [r.take(SLOTS, parts=FP1) for _ in range(2)]
        m1_h = [r.take(FT1, SLOTS, parts=FP1) for _ in range(2)]
        m1_outT = r.take(NB1, E1, CAP)
        m1_out = [r.take(3, D) for _ in range(2)]
        m1_x = r.take(NB1, D)
        m1_res = C[:, 0:NB1, :]
        X8 = X[:].rearrange("p (i b) d -> p i (b d)", b=NB1)

        def moe1_pe(pe):
            with pe.Fori(0, NIT1) as n:
                for b in range(NB1):
                    pe.wait_ge(m1.onehot, done(n, NB1 + 1, b + 2))
                    pe.wait_ge(m1.disp_sb, done(n, NB1, b - 1))
                    nc.tensor.matmul(bank[b % 2][:, 0:EC], m1_x[:, b, :],
                                     m1_hot[b % 2].rearrange("p e c -> p (e c)"), start=True, stop=True)\
                        .then_inc(m1.disp, 1)
                    pe.wait_ge(m1.combine, done(n, NB1, b + 1))
                    pe.wait_ge(m1.combT_sb, done(n, NB1, b - 1))
                    for c, (c0, m) in enumerate(CHUNKS):
                        last = nc.tensor.transpose(bank[2 + b % 2][0:m, c * T:(c + 1) * T],
                                                   m1_comb[b % 2][:, c0:c0 + m], ident[:])
                    last.then_inc(m1.combT, 1)
                pe.wait_ge(m1.disp_sb, done(n, NB1, NB1))
                pe.wait_ge(m1.combT_sb, done(n, NB1, NB1))
                for e in range(E1 + 1):
                    if e < E1:
                        for t in range(FT1):
                            k = e * FT1 + t
                            if k >= 2:
                                pe.wait_ge(m1.hidden, done(n, E1 * FT1, k - 1))
                            for j, w in enumerate((w1_l1, w3_l1)):
                                last = nc.tensor.matmul(bank[2 * (k % 2) + j][0:FP1, 0:SLOTS],
                                                        w[:, e, t * FP1:(t + 1) * FP1],
                                                        m1_disp[:, e, :, :].rearrange("p b c -> p (b c)"),
                                                        start=True, stop=True)
                            last.then_inc(m1.up, 1)
                    if e >= 1:
                        f = e - 1
                        pe.wait_ge(m1.hidden, done(n, E1 * FT1, (f + 1) * FT1))
                        pe.wait_ge(m1.down_sb, done(n, E1, f - 1))
                        for t in range(FT1):
                            last = nc.tensor.matmul(bank[4 + f % 2][:, 0:SLOTS], w2_l1[:, f, t, :],
                                                    m1_h[f % 2][:, t, :], start=(t == 0), stop=(t == FT1 - 1))
                        last.then_inc(m1.down, 1)
                pe.wait_ge(m1.down_sb, done(n, E1, E1))
                for b in range(NB1 + 1):
                    if b < NB1:
                        pe.wait_ge(m1.outT_sb, done(n, NB1, b - 1))
                        for c, (c0, m) in enumerate(CHUNKS):
                            last = nc.tensor.transpose(bank[b % 2][0:m, c * D:(c + 1) * D],
                                                       m1_outT[:, b, :, :].rearrange("p e c -> p (e c)")[:, c0:c0 + m],
                                                       ident[:])
                        last.then_inc(m1.outT, 1)
                    if b >= 1:
                        f = b - 1
                        pe.wait_ge(m1.outT_sb, done(n, NB1, f + 1))
                        pe.wait_ge(m1.res_sum, done(n, NB1, f - 1))
                        for c, (c0, m) in enumerate(CHUNKS):
                            last = nc.tensor.matmul(bank[6 + f % 2][:, 0:D], m1_combT[0:m, f, c, :],
                                                    m1_out[f % 2][0:m, c, :], start=(c == 0), stop=(c == 2))
                        last.then_inc(m1.y_ready, 1)

        def moe1_act(act):
            with act.Fori(0, NIT1) as n:
                for b in range(NB1):
                    act.wait_ge(m1.disp, done(n, NB1, b + 1))
                    nc.scalar.activation(m1_disp[:, :, b, :],
                                         bank[b % 2][:, 0:EC].rearrange("p (e c) -> p e c", e=E1), ACT.Copy)\
                        .then_inc(m1.disp_sb, 1)
                for k in range(E1 * FT1 + FT1):
                    e, t = k // FT1, k % FT1
                    if e < E1:
                        act.wait_ge(m1.up, done(n, E1 * FT1, k + 1))
                        act.wait_ge(m1.hidden, done(n, E1 * FT1, k - 1))
                        nc.scalar.activation(m1_s[k % 2], bank[2 * (k % 2)][0:FP1, 0:SLOTS], ACT.Silu)\
                            .then_inc(m1.silu, 1)
                    if e >= 1 and t == FT1 - 1:
                        act.wait_ge(m1.down, done(n, E1, e))
                        nc.scalar.activation(m1_outT[:, :, e - 1, :],
                                             bank[4 + (e - 1) % 2][:, 0:SLOTS].rearrange("p (b c) -> p b c", b=NB1),
                                             ACT.Copy).then_inc(m1.down_sb, 1)
                for b in range(NB1):
                    act.wait_ge(m1.outT, done(n, NB1, b + 1))
                    act.wait_ge(m1.y_ready, done(n, NB1, b - 1))
                    nc.scalar.activation(m1_out[b % 2][:, 0:2, :].rearrange("p c d -> p (c d)"),
                                         bank[b % 2][:, 0:2 * D], ACT.Copy)
                    m = CHUNKS[2][1]
                    nc.scalar.activation(m1_out[b % 2][0:m, 2, :], bank[b % 2][0:m, 2 * D:3 * D], ACT.Copy)\
                        .then_inc(m1.outT_sb, 1)

        def moe1_dve(dve):
            place8 = place1.rearrange("p (i b) e -> p i (b e)", b=NB1)
            probs8 = probs1.rearrange("p (i b) e -> p i (b e)", b=NB1)

            def norm(n):
                dve.wait_ge(m1.rstd, done(n, 1, 1))
                normalize(dve, m1, X8[:, n, :].rearrange("p (b d) -> p b d", b=NB1), m1_res, NB1)
                dve.drain()

            def body(n, behind):
                nc.vector.tensor_copy(m1_pl.rearrange("p b e -> p (b e)"), place8[:, n, :])
                nc.vector.tensor_copy(m1_x.rearrange("p b d -> p (b d)"), X8[:, n, :])
                nc.vector.tensor_copy(m1_p.rearrange("p b e -> p (b e)"), probs8[:, n, :])\
                    .then_inc(m1.onehot, 1)
                dve.drain()
                for b in range(NB1 + 1):
                    if b < NB1:
                        dve.wait_ge(m1.disp, done(n, NB1, b - 1))
                        dve.wait_ge(m1.combine, done(n, NB1, b - 1))
                        nc.vector.tensor_tensor(m1_hot[b % 2], m1_pl[:, b, :].unsqueeze(2).to_broadcast([128, E1, CAP]),
                                                slot[:, :].unsqueeze(1).to_broadcast([128, E1, CAP]), ALU.is_equal)\
                            .then_inc(m1.onehot, 1)
                    if b >= 1:
                        f = b - 1
                        dve.wait_ge(m1.combT, done(n, NB1, f + 1))
                        nc.vector.tensor_copy(m1_combT[:, f, 0:2, :].rearrange("p c t -> p (c t)"),
                                              bank[2 + f % 2][:, 0:2 * T])
                        m = CHUNKS[2][1]
                        nc.vector.tensor_copy(m1_combT[0:m, f, 2, :], bank[2 + f % 2][0:m, 2 * T:3 * T])\
                            .then_inc(m1.combT_sb, 1)
                if behind:
                    norm_stats(dve, m1, m1_res, NB1)
                for k in range(E1 * FT1):
                    e, t = k // FT1, k % FT1
                    if behind and k == 2 * FT1:
                        norm(n - 1)
                    dve.wait_ge(m1.silu, done(n, E1 * FT1, k + 1))
                    if t == 0 and e >= 2:
                        dve.wait_ge(m1.down, done(n, E1, e - 1))
                    nc.vector.tensor_tensor(m1_h[e % 2][:, t, :], m1_s[k % 2], bank[2 * (k % 2) + 1][0:FP1, 0:SLOTS],
                                            ALU.mult).then_inc(m1.hidden, 1)
                for b in range(NB1):
                    dve.wait_ge(m1.y_ready, done(n, NB1, b + 1))
                    nc.vector.tensor_tensor(m1_res[:, b, :], bank[6 + b % 2][:, 0:D], m1_x[:, b, :], ALU.add)\
                        .then_inc(m1.res_sum, 1)
                dve.drain()
            body(0, False)
            with dve.Fori(1, NIT1) as n:
                body(n, True)
            norm_stats(dve, m1, m1_res, NB1)
            norm(NIT1 - 1)

        def moe1_pool(pool):
            def inv(n):
                pool.wait_ge(m1.stats, done(n, 1, 1))
                inv_std(pool, m1, NB1, lneps[:, 0:1].to_broadcast([128, NB1]), mv[:, 0:NB1, 1])

            def body(n):
                for b in range(NB1):
                    pool.wait_ge(m1.onehot, done(n, NB1 + 1, b + 2))
                    pool.wait_ge(m1.combT, done(n, NB1, b - 1))
                    nc.gpsimd.tensor_tensor(m1_comb[b % 2].rearrange("p (e c) -> p e c", e=E1), m1_hot[b % 2],
                                            m1_p[:, b, :].unsqueeze(2).to_broadcast([128, E1, CAP]), ALU.mult)\
                        .then_inc(m1.combine, 1)
            body(0)
            with pool.Fori(1, NIT1) as n:
                body(n)
                inv(n - 1)
            inv(NIT1 - 1)

        def moe1_sp(sp, out_v):
            with sp.Fori(0, NIT1) as n:
                sp.wait_ge(m1.normed, done(n, 1, 1))
                sp.dma_start(out_v[n], X8[:, n, :].rearrange("p (b d) -> p b d", b=NB1)).then_inc(stored, 16)
            sp.wait_ge(stored, 16 * NIT1)

        blk = ctx.enter_context(nc.Block())
        x_v = ins["x"].rearrange("b t d -> t b d")
        ctx_v = ins["ctx"].rearrange("b t d -> t b d")

        N_CONST, N_MIX, N_SMALL, N_FF, N_ROWS = 6, 5, 4, 6, len(rows) + len(cols) - 5

        @blk.sync
        def _(sp):
            issued = dict.fromkeys(loaded, 0)

            def load(dst, src, what):
                issued[what] += 1
                sp.dma_start(dst, src).then_inc(loaded[what], 16)
            load(ident[:, :], ins["c_ident"], "consts")
            load(X[:], x_v, "x")
            load(w_rwkv, ins["rwkv_w"].rearrange("n c o -> c n o"), "rwkv")
            for k in ("decay", "first", "mix_k", "mix_v", "mix_r"):
                load(cols[k][:, :], ins[k], "mix")
            for j in range(2):
                load(mask32[j], ins["mask"][:, j * B * T // 8:(j + 1) * B * T // 8], "mask")
            load(headmask[:, :], ins["c_headmask"], "consts")
            load(cosr[:, :], ins["c_cos"], "consts")
            load(sinr[:, :], ins["c_sin"], "consts")
            load(slot[:, :], ins["c_slot"], "consts")
            load(rank[:, :], ins["c_rank"], "consts")
            for a, p in enumerate(("sa", "ca")):
                for k, w in enumerate(("wq", "wk", "wv")):
                    load(w_att[a][k], ins[f"{p}_{w}"], "attention")
                load(w_att[a][3].rearrange("p (t d) -> p t d", d=D),
                     ins[f"{p}_wo"].rearrange("(t p) d -> p t d", p=128), "attention")
            for k, dram in (("sa_bo", "sa_bo"), ("ca_bo", "ca_bo"), ("ln1_g", "ln1_g"), ("ln1_b", "ln1_b"),
                            ("ln2_g", "ln2_g"), ("ln2_b", "ln2_b"), ("ln3_g", "ln3_g"), ("ln3_b", "ln3_b"),
                            ("fc2_b", "fc2_b"), ("norm_w", "norm_w"), ("l1_bqkv", "l1_bqkv"), ("l1_bo", "l1_bo"),
                            ("l1x_bv", "l1x_bv")):
                n = rows[k].shape[1]
                load(rows[k][:, :], ins[dram].unsqueeze(0).to_broadcast([128, n]), "rows")
            for k in ("fc1_b", "b1", "l1x_bq", "l1x_bk"):
                load(cols[k][:, :], ins[k], "rows")
            load(C[:], ctx_v, "ctx")
            load(fc1, ins["fc1_w"], "ff")
            load(fc2, ins["fc2_w"].rearrange("(t p) m -> p t m", p=128), "ff")
            load(w1_l0, ins["moe0_w1"].rearrange("e c f -> c e f"), "ff")
            load(w2_l0, ins["moe0_w2"].rearrange("e (t p) m -> p e t m", p=128), "ff")
            load(gate0[:, :], ins["gate0"], "ff")
            load(b2_sb[:, :], ins["b2"], "ff")
            load(w_l1[:, 0:QKV], ins["l1_wqkv"], "small")
            load(w_l1[:, QKV:QKV + D], ins["l1_wo"], "small")
            load(w_l1x, ins["l1x_w"].rearrange("n c o -> c n o"), "small")
            load(gate1[:, :], ins["gate1"], "small")
            sp.wait_ge(stage_end, 4 * 3)
            load(w1_l1, ins["moe1_w1"].rearrange("e c f -> c e f"), "moe1_w13")
            load(w3_l1, ins["moe1_w3"].rearrange("e c f -> c e f"), "moe1_w13")
            sp.wait_ge(stage_end, 4 * 6)
            load(w2_l1, ins["moe1_w2"].rearrange("e (t p) m -> p e t m", p=FP1), "moe1_w2")
            prime(sp, "sp")
            sp.wait_ge(stage_end, 4 * 7)
            attnx_sp(sp, ins["mask_l1"].rearrange("(i b) q k -> i q b k", b=NB))
            for k, t in loaded.items():
                sp.wait_ge(t, 16 * issued[k])
            sp.wait_ge(stage_end, 4 * 9)
            moe1_sp(sp, out.rearrange("(i b) t d -> i t b d", b=NB1))

        @blk.gpsimd
        def _(pool):
            prime(pool, "pool")
            nc.gpsimd.memset(half[:, :], -0.5)
            nc.gpsimd.memset(lneps[:, :], LN_EPS)
            nc.gpsimd.memset(rmseps[:, :], RMS_EPS)
            nc.gpsimd.memset(carry[:, :], 0.0)
            nc.gpsimd.memset(onerow[:, :], 0.0)
            nc.gpsimd.memset(keymask[:, :], 0.0)
            pool.drain()
            nc.gpsimd.memset(onerow[0:1, :], 1.0)
            nc.gpsimd.memset(upper[:, :], 1.0)
            for t in (rk_xx[0], rk_xx[1], rk_ek[0], rk_ek[1], rk_ekv, rk_ew):
                last = nc.gpsimd.memset(t, 0.0)
            pool.drain()
            nc.gpsimd.affine_select(out=upper[:, :], in_=upper[:, :], compare_op=ALU.is_ge, fill=0.0, base=0,
                                    pattern=[[1, 128]], channel_multiplier=-1)
            pool.drain().then_inc(setup_done, 1)
            pool.wait_ge(loaded["x"], 16)
            rwkv_pool(pool)
            end_stage(pool, 0)
            nc.gpsimd.memset(at_v[:, :, :, DH0], 1.0)
            pool.drain()
            end_stage(pool, 1)
            pool.wait_ge(loaded["rows"], 16 * N_ROWS)
            pool.wait_ge(loaded["consts"], 16 * N_CONST)
            pool.wait_ge(loaded["ctx"], 16)
            attention_pool(pool, 0)
            pool.drain()
            attention_pool(pool, 1)
            end_stage(pool, 2)
            ffn_pool(pool)
            end_stage(pool, 3)
            router0_pool(pool)
            end_stage(pool, 4)
            moe0_pool(pool)
            end_stage(pool, 5)
            for v in l1_v:
                nc.gpsimd.memset(v[:, :, :, DH1], 1.0)
            pool.drain()
            attn1_pool(pool)
            end_stage(pool, 6)
            attnx_pool(pool)
            end_stage(pool, 7)
            router1_pool(pool)
            end_stage(pool, 8)
            moe1_pool(pool)

        @blk.tensor
        def _(pe):
            prime(pe, "pe")
            pe.wait_ge(loaded["consts"], 16 * N_CONST)
            pe.wait_ge(loaded["x"], 16)
            pe.wait_ge(setup_done, 3)
            rwkv_pe(pe)
            end_stage(pe, 0)
            end_stage(pe, 1)
            pe.wait_ge(loaded["attention"], 16 * 8)
            attention_pe(pe, 0)
            pe.wait_ge(loaded["ctx"], 16)
            pe.wait_ge(at.affine, done(NIT, 1, 0))
            attention_pe(pe, 1)
            end_stage(pe, 2)
            pe.wait_ge(loaded["ff"], 16 * N_FF)
            ffn_pe(pe)
            end_stage(pe, 3)
            router0_pe(pe)
            end_stage(pe, 4)
            moe0_pe(pe)
            end_stage(pe, 5)
            pe.wait_ge(loaded["small"], 16 * N_SMALL)
            attn1_pe(pe)
            end_stage(pe, 6)
            attnx_pe(pe)
            end_stage(pe, 7)
            router1_pe(pe)
            end_stage(pe, 8)
            pe.wait_ge(loaded["moe1_w13"], 32)
            pe.wait_ge(loaded["moe1_w2"], 16)
            moe1_pe(pe)

        @blk.scalar
        def _(act):
            prime(act, "act")
            act.wait_ge(loaded["mix"], 16 * N_MIX)
            act.wait_ge(setup_done, 1)
            nc.scalar.activation(rk_ewc, cols["decay"][:, :], ACT.Exp, scale=1.0 / T)
            nc.scalar.activation(rk_u, cols["first"][:, :], ACT.Copy, scale=1.0 / T)
            act.drain()
            nc.scalar.activation(rk_ew[:, :, 1:T], rk_ew[:, :, 1:T], ACT.Identity, bias=rk_ewc[:, 0:1])
            act.drain().then_inc(setup_done, 1)
            rwkv_act(act)
            end_stage(act, 0)
            end_stage(act, 1)
            act.wait_ge(loaded["rows"], 16 * N_ROWS)
            attention_act(act, 0)
            attention_act(act, 1)
            end_stage(act, 2)
            ffn_act(act)
            end_stage(act, 3)
            router0_act(act)
            end_stage(act, 4)
            moe0_act(act)
            end_stage(act, 5)
            attn1_act(act)
            end_stage(act, 6)
            attnx_act(act)
            end_stage(act, 7)
            router1_act(act)
            end_stage(act, 8)
            moe1_act(act)

        @blk.vector
        def _(dve):
            prime(dve, "dve")
            dve.wait_ge(loaded["mix"], 16 * N_MIX)
            dve.wait_ge(loaded["rwkv"], 16)
            dve.wait_ge(setup_done, 1)
            dve.wait_ge(loaded["mask"], 32)
            for j in range(2):
                nc.vector.tensor_scalar(keymask[0:1, j * B * T // 2:(j + 1) * B * T // 2],
                                        mask8[j], MASKED, None, ALU.mult)
            for k, m in enumerate(("mix_k", "mix_v", "mix_r")):
                nc.vector.tensor_scalar(rk_onem[:, k:k + 1], cols[m][:, :], -1.0, 1.0, ALU.mult, ALU.add)
            dve.drain()
            for k, m in enumerate(("mix_k", "mix_v", "mix_r")):
                nc.vector.tensor_scalar(rk_scaled[:, k, 0, :], w_rwkv[:, k, :], cols[m][:, 0:1], None, ALU.mult)
                nc.vector.tensor_scalar(rk_scaled[:, k, 1, :], w_rwkv[:, k, :], rk_onem[:, k:k + 1], None, ALU.mult)
            dve.wait_ge(setup_done, 2)
            dve.wait_ge(loaded["x"], 16)
            dve.drain().then_inc(setup_done, 1)
            rwkv_dve(dve)
            end_stage(dve, 0)
            end_stage(dve, 1)
            dve.wait_ge(loaded["consts"], 16 * N_CONST)
            dve.wait_ge(loaded["rows"], 16 * N_ROWS)
            attention_dve(dve, 0)
            attention_dve(dve, 1)
            end_stage(dve, 2)
            ffn_dve(dve)
            end_stage(dve, 3)
            router0_dve(dve)
            end_stage(dve, 4)
            moe0_dve(dve)
            end_stage(dve, 5)
            attn1_dve(dve)
            end_stage(dve, 6)
            attnx_dve(dve)
            end_stage(dve, 7)
            router1_dve(dve)
            end_stage(dve, 8)
            moe1_dve(dve)


def kernel(**inputs):
    import numpy as np
    import concourse.bacc as bacc
    from concourse.bass_utils import run_bass_kernel_spmd

    a = {k: np.asarray(v) for k, v in inputs.items()}
    t = lambda name: np.ascontiguousarray(a[name].T)
    col = lambda name: np.ascontiguousarray(a[name].reshape(-1, 128).T)
    swap = lambda name: np.ascontiguousarray(np.swapaxes(a[name], 1, 2))
    arrays = {
        "x": a["x"], "ctx": a["ctx_1024"],
        "mask": a["mask_BxS2_bk0"].reshape(1, -1).view(np.int32),
        "mask_l1": a["mask_Bx1xSxS2_ik1"].reshape(32, 128, 128),
        "rwkv_w": np.stack([t("L0_attn_Wk"), t("L0_attn_Wv"), t("L0_attn_Wr"), t("L0_attn_Wo")]),
        "decay": col("L0_attn_spatial_decay"), "first": col("L0_attn_spatial_first"),
        "mix_k": col("L0_attn_mix_k"), "mix_v": col("L0_attn_mix_v"), "mix_r": col("L0_attn_mix_r"),
        "fc1_w": a["L0_xattn_fc1_w"], "fc1_b": col("L0_xattn_fc1_b"),
        "fc2_w": a["L0_xattn_fc2_w"], "fc2_b": a["L0_xattn_fc2_b"],
        "norm_w": a["L0_ffn_norm_weight"], "gate0": t("L0_ffn_gate_w"),
        "moe0_w1": swap("L0_ffn_w1"), "b1": col("L0_ffn_b1"),
        "moe0_w2": swap("L0_ffn_w2"), "b2": a["L0_ffn_b2"],
        "l1_wqkv": np.concatenate([a["L1_attn_Wq"], a["L1_attn_Wk"], a["L1_attn_Wv"]], axis=1),
        "l1_bqkv": np.concatenate([a["L1_attn_bq"], a["L1_attn_bk"], a["L1_attn_bv"]]),
        "l1_wo": a["L1_attn_Wo"], "l1_bo": a["L1_attn_bo"],
        "l1x_w": np.stack([t("L1_xattn_Wq"), t("L1_xattn_Wk"), t("L1_xattn_Wv"), t("L1_xattn_Wo")]),
        "l1x_bq": col("L1_xattn_bq"), "l1x_bk": col("L1_xattn_bk"), "l1x_bv": a["L1_xattn_bv"],
        "gate1": t("L1_ffn_gate_w"), "moe1_w1": a["L1_ffn_w1"], "moe1_w3": a["L1_ffn_w3"], "moe1_w2": a["L1_ffn_w2"],
    }
    for p in ("sa", "ca"):
        for w in ("wq", "wk", "wv", "wo", "bo"):
            arrays[f"{p}_{w}"] = a[f"L0_xattn_{p}_{w}"]
    for k in (1, 2, 3):
        for w in ("g", "b"):
            arrays[f"ln{k}_{w}"] = a[f"L0_xattn_ln{k}_{w}"]
    f32 = np.float32
    freq = f32(1.0) / f32(10000.0) ** (np.arange(0, 8, 2, dtype=f32) / f32(8))
    angle = (np.arange(128, dtype=f32)[:, None] * freq[None, :]).astype(f32)
    arrays["c_cos"] = np.concatenate([np.cos(angle)] * 2, axis=1).astype(f32)
    arrays["c_sin"] = np.concatenate([np.sin(angle)] * 2, axis=1).astype(f32)
    arrays["c_ident"] = np.eye(128, dtype=f32)
    arrays["c_headmask"] = np.repeat(np.eye(16, dtype=f32), 8, axis=0)
    arrays["c_slot"] = np.tile(np.arange(1, 41, dtype=f32), (128, 1))
    arrays["c_rank"] = np.tile(np.arange(8, 0, -1).astype(f32), (128, 1))

    nc = bacc.Bacc("TRN2", target_bir_lowering=False, num_devices=1)
    ins, feed = {}, {}
    for name, v in arrays.items():
        v = np.ascontiguousarray(v)
        feed["in_" + name] = v
        ins[name] = nc.dram_tensor("in_" + name, v.shape, mybir.dt.from_np(v.dtype), kind="ExternalInput").ap()
    out = nc.dram_tensor("out", (32, 128, 128), mybir.dt.float32, kind="ExternalOutput").ap()
    build(nc, ins, out)
    result = run_bass_kernel_spmd(nc, [feed], core_ids=[0])
    return result.results[0]["out"]
```
